# Optimizing a Trainium2 kernel written in Bass

```python
import numpy as np
import jax
import jax.numpy as jnp

def _softmax(x, axis=-1):
    return jax.nn.softmax(x, axis=axis)

def _gelu(x):
    return jax.nn.gelu(x, approximate=True)

def _silu(x):
    return jax.nn.silu(x)

def _sigmoid(x):
    return jax.nn.sigmoid(x)

def _layernorm(x, axis=-1, eps=1e-05):
    m = jnp.mean(x, axis=axis, keepdims=True)
    v = jnp.var(x, axis=axis, keepdims=True)
    return (x - m) / jnp.sqrt(v + eps)

def _scatter_add(tgt, idx, src, axis=0):
    return tgt.at[idx].add(src)

def _segment_sum(src, seg, n):
    return jax.ops.segment_sum(src, seg, n)
kernel_name = 'mk_prb_d1_jaxref_r4_da2450'

def setup_inputs(seed: int=0):
    np.random.seed(seed)
    _w = jnp.asarray

    def _L0_attn_setup():
        import jax, jax.numpy as jnp
        import numpy as np
        EMBED_DIM = 256
        NUM_HEADS = 16
        HEAD_DIM = EMBED_DIM // NUM_HEADS

        def _sinusoid_pos_emb(seq_len, dim):
            pos = jnp.arange(seq_len, dtype=jnp.float32)
            idx = jnp.arange(dim // 2, dtype=jnp.float32)
            inv_freq = 1.0 / 10000.0 ** (2.0 * idx / dim)
            ang = pos[:, None] * inv_freq[None, :]
            return jnp.concatenate([jnp.sin(ang), jnp.cos(ang)], axis=-1)

        def _relative_shift(x):
            b, h, s, _ = x.shape
            x = jnp.pad(x, ((0, 0), (0, 0), (0, 0), (1, 0)))
            x = x.reshape(b, h, s + 1, s)
            return x[:, :, 1:, :].reshape(b, h, s, s)
        key = jax.random.key(seed)
        ks = jax.random.split(key, 12)
        D = EMBED_DIM
        sc = 1.0 / np.sqrt(D)
        inp = {'x': jax.random.normal(ks[0], (2, 512, D), dtype=jnp.float32)}
        for i, name in enumerate(['Wq', 'Wk', 'Wv', 'Wp', 'Wo']):
            inp[name] = jax.random.normal(ks[1 + i], (D, D), dtype=jnp.float32) * sc
            inp['b' + name[1].lower()] = jnp.zeros((D,), dtype=jnp.float32)
        inp['u'] = jax.random.normal(ks[6], (1, NUM_HEADS, 1, HEAD_DIM), dtype=jnp.float32) * 0.05
        inp['v'] = jax.random.normal(ks[7], (1, NUM_HEADS, 1, HEAD_DIM), dtype=jnp.float32) * 0.05
        return inp
    _L0_attn_in = _L0_attn_setup()

    def _L0_ffn_setup():
        import jax, jax.numpy as jnp
        import numpy as np
        N, T, D = (4, 1024, 256)
        NUM_EXPERTS = 8
        EXPERT_CAP = 2.0
        MLP_RATIO = 4
        HIDDEN = MLP_RATIO * D
        key = jax.random.key(seed)
        k1, k2, k3, k4 = jax.random.split(key, 4)
        x = jax.random.normal(k1, (N, T, D), dtype=jnp.float32)
        gate_w = jax.random.truncated_normal(k2, -2.0, 2.0, (D, NUM_EXPERTS), dtype=jnp.float32) * 0.02
        w1 = jax.random.normal(k3, (NUM_EXPERTS, D, HIDDEN), dtype=jnp.float32) * 0.02
        w2 = jax.random.normal(k4, (NUM_EXPERTS, HIDDEN, D), dtype=jnp.float32) * 0.02
        return {'x': x, 'gate_w': gate_w, 'w1': w1, 'w2': w2}
    _L0_ffn_in = _L0_ffn_setup()
    _d = {'L0_attn_x': _L0_attn_in['x'], 'L0_attn_Wq': _L0_attn_in['Wq'], 'L0_attn_bq': _L0_attn_in['bq'], 'L0_attn_Wk': _L0_attn_in['Wk'], 'L0_attn_bk': _L0_attn_in['bk'], 'L0_attn_Wv': _L0_attn_in['Wv'], 'L0_attn_bv': _L0_attn_in['bv'], 'L0_attn_Wp': _L0_attn_in['Wp'], 'L0_attn_bp': _L0_attn_in['bp'], 'L0_attn_Wo': _L0_attn_in['Wo'], 'L0_attn_bo': _L0_attn_in['bo'], 'L0_attn_u': _L0_attn_in['u'], 'L0_attn_v': _L0_attn_in['v'], 'L0_ffn_gate_w': _L0_ffn_in['gate_w'], 'L0_ffn_w1': _L0_ffn_in['w1'], 'L0_ffn_w2': _L0_ffn_in['w2']}
    _x0 = _d['L0_attn_x']
    _d['L0_attn_x'] = jax.random.normal(jax.random.fold_in(jax.random.key(seed), 1), (32, 512, 256), dtype=_x0.dtype)
    del _x0
    return _d

def reference(L0_attn_x, L0_attn_Wq, L0_attn_bq, L0_attn_Wk, L0_attn_bk, L0_attn_Wv, L0_attn_bv, L0_attn_Wp, L0_attn_bp, L0_attn_Wo, L0_attn_bo, L0_attn_u, L0_attn_v, L0_ffn_gate_w, L0_ffn_w1, L0_ffn_w2):

    def _L0_attn_ref(x, Wq, bq, Wk, bk, Wv, bv, Wp, bp, Wo, bo, u, v):
        import jax, jax.numpy as jnp
        import numpy as np
        EMBED_DIM = 256
        NUM_HEADS = 16
        HEAD_DIM = EMBED_DIM // NUM_HEADS

        def _sinusoid_pos_emb(seq_len, dim):
            pos = jnp.arange(seq_len, dtype=jnp.float32)
            idx = jnp.arange(dim // 2, dtype=jnp.float32)
            inv_freq = 1.0 / 10000.0 ** (2.0 * idx / dim)
            ang = pos[:, None] * inv_freq[None, :]
            return jnp.concatenate([jnp.sin(ang), jnp.cos(ang)], axis=-1)

        def _relative_shift(x):
            b, h, s, _ = x.shape
            x = jnp.pad(x, ((0, 0), (0, 0), (0, 0), (1, 0)))
            x = x.reshape(b, h, s + 1, s)
            return x[:, :, 1:, :].reshape(b, h, s, s)
        B, S, D = x.shape
        H, P = (NUM_HEADS, HEAD_DIM)

        def heads(t):
            return t.reshape(B, S, H, P).transpose(0, 2, 1, 3)
        q = heads(x @ Wq + bq)
        k = heads(x @ Wk + bk)
        val = heads(x @ Wv + bv)
        pos = _sinusoid_pos_emb(S, D) @ Wp + bp
        pos = pos.reshape(S, H, P).transpose(1, 0, 2)
        content_score = jnp.einsum('bhsp,bhtp->bhst', q + u, k)
        pos_score = jnp.einsum('bhsp,htp->bhst', q + v, pos)
        pos_score = _relative_shift(pos_score)
        score = (content_score + pos_score) / jnp.sqrt(jnp.float32(P))
        weights = jax.nn.softmax(score, axis=-1)
        out = jnp.einsum('bhst,bhtp->bhsp', weights, val)
        out = out.transpose(0, 2, 1, 3).reshape(B, S, D)
        return out @ Wo + bo

    def _L0_ffn_ref(x, gate_w, w1, w2):
        import jax, jax.numpy as jnp
        import numpy as np
        N, T, D = (4, 1024, 256)
        NUM_EXPERTS = 8
        EXPERT_CAP = 2.0
        MLP_RATIO = 4
        HIDDEN = MLP_RATIO * D
        x = x.astype(jnp.float32)
        n, t, d = x.shape
        k = int(EXPERT_CAP * t / NUM_EXPERTS)
        scores = jnp.einsum('ntd,de->nte', x, gate_w)
        probs = jax.nn.softmax(scores, axis=-1)
        probs = jnp.transpose(probs, (0, 2, 1))
        g, m = jax.lax.top_k(probs, k)
        xin = jax.vmap(lambda xb, mb: xb[mb])(x, m)
        h = jax.nn.gelu(jnp.einsum('nekd,edf->nekf', xin, w1))
        h = jnp.einsum('nekf,efd->nekd', h, w2)
        weighted = g[..., None] * h
        flat_idx = (m + jnp.arange(n, dtype=m.dtype)[:, None, None] * t).reshape(-1)
        out = jnp.zeros((n * t, d), dtype=jnp.float32).at[flat_idx].add(weighted.reshape(-1, d))
        out = out.reshape(n, t, d)
        return out.astype(jnp.bfloat16)
    x = L0_attn_x
    xn = _layernorm(x, axis=-1)
    x = x + _L0_attn_ref(xn, L0_attn_Wq, L0_attn_bq, L0_attn_Wk, L0_attn_bk, L0_attn_Wv, L0_attn_bv, L0_attn_Wp, L0_attn_bp, L0_attn_Wo, L0_attn_bo, L0_attn_u, L0_attn_v) + _L0_ffn_ref(xn, L0_ffn_gate_w, L0_ffn_w1, L0_ffn_w2)
    return x

_drawn_inputs = setup_inputs


def setup_inputs(seed=0):
    import zlib

    import numpy as np

    out = dict(_drawn_inputs(seed))
    spreads = {'L0_attn_bq': (0.0, 0.747),
     'L0_attn_bk': (0.0, 0.8),
     'L0_attn_bv': (0.0, 0.1),
     'L0_attn_bp': (0.0, 0.8),
     'L0_attn_bo': (0.0, 0.1)}
    factors = {'L0_attn_u': 8.0, 'L0_attn_v': 8.0}
    for name, (base, spread) in spreads.items():
        noise = np.random.default_rng([zlib.crc32(name.encode()), seed]).standard_normal(out[name].shape)
        drawn = base * np.exp(spread * noise) if base else spread * noise
        out[name] = jnp.asarray(drawn.astype(out[name].dtype))
    for name, factor in factors.items():
        out[name] = (out[name] * factor).astype(out[name].dtype)
    return out
```

```python
from contextlib import ExitStack

import numpy as np

import concourse.bass as bass
from concourse import mybir

ALU = mybir.AluOpType
ACT = mybir.ActivationFunctionType
F32 = mybir.dt.float32
F32R = mybir.dt.float32r
BF16 = mybir.dt.bfloat16
AX_X = mybir.AxisListType.X

P = 128
D = 256
DC = D // P
B = 32
S = 512
TT = S // P
H = 16
HD = D // H
NQ = 4
QH = H // NQ
NE = 8
F = 1024
FC = F // P
CAP = 2 * S // NE
HALF = B // 2
GB = 4
NG = B // GB
EPS = 1e-5
NEG = -3.0e38
SPLITS = ((0, 0), (0, 1), (1, 0))


def wait(eng, sem, value):
    if isinstance(value, int) and value <= 0:
        return
    eng.wait_ge(sem, value)


def wait_alone(eng, sem, value):
    wait(eng, sem, value)
    if not isinstance(value, int):
        eng.nop(nofuse=True)


def first_apart(eng, n, body):
    body(0)
    with eng.Fori(1, n) as i:
        body(i)


def ends_apart(eng, n, body):
    body(0)
    with eng.Fori(1, n - 1) as i:
        body(i)
    body(n - 1)


class Memory:

    def __init__(self, nc, ctx, phase):
        self.nc, self.ctx, self.phase = nc, ctx, phase

    def sb(self, name, shape, dt=F32):
        return self.ctx.enter_context(self.nc.sbuf_tensor(f"{self.phase}_{name}", shape, dt))

    def ps(self, name, shape):
        return self.ctx.enter_context(self.nc.psum_tensor(f"{self.phase}_{name}", shape, F32))

    def sem(self, name):
        return self.ctx.enter_context(self.nc.semaphore(f"{self.phase}_{name}"))


def shape_constants():
    pos = np.arange(S, dtype=np.float32)
    idx = np.arange(D // 2, dtype=np.float32)
    inv = (np.float32(1.0) / np.float32(10000.0) ** (np.float32(2.0) * idx / np.float32(D))).astype(np.float32)
    ang = (pos[:, None] * inv[None, :]).astype(np.float32)
    sinusoid = np.ascontiguousarray(np.concatenate([np.sin(ang), np.cos(ang)], axis=-1).astype(np.float32).T)
    ident = np.eye(P, dtype=np.float32)
    spread = np.zeros((P, P), np.float32)
    for q in range(4):
        spread[32 * q + HD, 32 * q:32 * q + 32] = 1.0
    slots = np.tile(np.arange(CAP, dtype=np.float32), (P, 1))
    slot_col = np.arange(P, dtype=np.float32).reshape(P, 1)
    keep = np.zeros((P, QH), np.float32)
    for hh in range(QH):
        for part in range(2):
            keep[64 * part + HD * hh:64 * part + HD * (hh + 1), hh] = 1.0
    return sinusoid, ident, spread, slots, slot_col, keep


def norm_phase(nc, x, gate_w, ident_d, xn_d, xt_d, gate):
    with ExitStack() as ctx:
        m = Memory(nc, ctx, "norm")
        ident = m.sb("ident", [P, P])
        gw = m.sb("gw", [P, DC, NE])
        gws = m.sb("gws", [P, 2, DC, NE], F32R)
        xin = m.sb("xin", [P, 2, TT, D])
        xn = m.sb("xn", [P, 2, TT, D])
        stats = m.sb("stats", [P, 2, TT, 6])
        mv = m.sb("mv", [P, 2, TT, 2])
        sd = m.sb("sd", [P, 2, TT])
        rstd = m.sb("rstd", [P, 2, TT])
        eps = m.sb("eps", [P, 1])
        xts = m.sb("xts", [P, 2, 2, DC, S], F32R)
        tp = m.ps("tp", [P, 2, DC, S])
        gp = m.ps("gp", [P, 2, S])
        const_in = m.sem("const_in")
        split = m.sem("split")
        x_in = [m.sem(f"x_in{s}") for s in range(2)]
        stat = m.sem("stat")
        aggr = m.sem("aggr")
        root = m.sem("root")
        recip = m.sem("recip")
        normed = m.sem("normed")
        turned = m.sem("turned")
        high = m.sem("high")
        low = m.sem("low")
        scored = m.sem("scored")
        kept = m.sem("kept")
        stored = [m.sem(f"stored{s}") for s in range(2)]

        with nc.Block() as block:

            @block.sync
            def _(sp):
                sp.dma_start(ident[:, :], ident_d).then_inc(const_in, 16)
                sp.dma_start(gw[:, :, :], gate_w.rearrange("(c p) e -> p c e", p=P)).then_inc(const_in, 16)

                def body(i):
                    for s in range(2):
                        b = i * 2 + s
                        wait_alone(sp, normed, b - 1)
                        sp.dma_start(xin[:, s], x[bass.ds(b, 1)].rearrange("o (t p) d -> p (o t) d", p=P)).then_inc(x_in[s], 16)

                first_apart(sp, B // 2, body)

            @block.gpsimd
            def _(pool):
                def body(i):
                    for s in range(2):
                        b = i * 2 + s
                        wait_alone(pool, normed, b + 1)
                        pool.dma_start(xn_d[bass.ds(b, 1)].rearrange("o p t d -> p (o t) d"), xn[:, s]).then_inc(stored[s], 16)
                        wait_alone(pool, low, b + 1)
                        pool.dma_start(xt_d[bass.ds(b, 1)].rearrange("o p k c t -> p (o k) c t"), xts[:, s].bitcast(F32)).then_inc(stored[s], 16)

                first_apart(pool, B // 2, body)
                for s in range(2):
                    wait_alone(pool, stored[s], 32 * (B // 2))

            @block.vector
            def _(dve):
                dve.memset(eps[:, :], EPS).then_inc(split, 1)
                dve.wait_ge(const_in, 32)
                dve.tensor_copy(gws[:, 0], gw[:, :, :]).then_inc(split, 1)
                dve.wait_ge(split, 2)
                dve.tensor_tensor(gws[:, 1], gw[:, :, :], gws[:, 0].bitcast(F32), ALU.subtract).then_inc(split, 1)

                def body(i):
                    for s in range(2):
                        b = i * 2 + s
                        dve.wait_ge(x_in[s], (i + 1) * 16)
                        for t in range(TT):
                            dve.bn_stats(stats[:, s, t], xin[:, s, t]).then_inc(stat, 1)
                        wait_alone(dve, stat, (b + 1) * TT)
                        for t in range(TT):
                            dve.bn_aggr(mv[:, s, t], stats[:, s, t]).then_inc(aggr, 1)
                        dve.wait_ge(root, b + 1)
                        dve.reciprocal(rstd[:, s], sd[:, s]).then_inc(recip, 1)
                        dve.wait_ge(recip, b + 1)
                        wait(dve, stored[s], i * 32)
                        wait(dve, turned, b - 1)
                        for t in range(TT):
                            ins = dve.tensor_scalar(xn[:, s, t], xin[:, s, t], mv[:, s, t, 0:1], rstd[:, s, t:t + 1],
                                                    ALU.subtract, ALU.mult)
                        ins.then_inc(normed, 1)
                        dve.wait_ge(high, b + 1)
                        dve.tensor_tensor(xts[:, s, 1], tp[:, s], xts[:, s, 0].bitcast(F32), ALU.subtract).then_inc(low, 1)

                first_apart(dve, B // 2, body)

            @block.scalar
            def _(act):
                act.wait_ge(split, 1)

                def body(i):
                    for s in range(2):
                        b = i * 2 + s
                        act.wait_ge(aggr, (b + 1) * TT)
                        act.activation(sd[:, s], mv[:, s, :, 1], ACT.Sqrt, bias=eps[:, :]).then_inc(root, 1)
                        act.wait_ge(turned, b + 1)
                        wait(act, stored[s], i * 32)
                        wait(act, scored, b - 1)
                        act.activation(xts[:, s, 0], tp[:, s], ACT.Copy).then_inc(high, 1)
                        act.wait_ge(scored, b + 1)
                        act.activation(gate[:, bass.ds(b, 1)], gp[:, s:s + 1, 0:TT * NE].rearrange("p o (t e) -> p o t e", e=NE),
                                       ACT.Copy).then_inc(kept, 1)

                first_apart(act, B // 2, body)

            @block.tensor
            def _(pe):
                pe.wait_ge(const_in, 32)
                pe.wait_ge(split, 3)

                def body(i):
                    for s in range(2):
                        b = i * 2 + s
                        pe.wait_ge(normed, b + 1)
                        wait(pe, low, b - 1)
                        for c in range(DC):
                            for t in range(TT):
                                ins = pe.transpose(tp[:, s, c, t * P:(t + 1) * P], xn[:, s, t, c * P:(c + 1) * P], ident[:, :])
                        ins.then_inc(turned, 1)
                        pe.wait_ge(low, b + 1)
                        wait(pe, kept, b - 1)
                        for t in range(TT):
                            for k, (w, a) in enumerate(SPLITS):
                                for c in range(DC):
                                    ins = pe.matmul(gp[:, s, t * NE:(t + 1) * NE], xts[:, s, a, c, t * P:(t + 1) * P],
                                                    gws[:, w, c, :], start=(k == 0 and c == 0), stop=(k == 2 and c == DC - 1))
                        ins.then_inc(scored, 1)

                first_apart(pe, B // 2, body)


def route_phase(nc, ident_d, gate, slot_t, slot_d, prob_d):
    R = HALF * NE
    with ExitStack() as ctx:
        m = Memory(nc, ctx, "route")
        ident = m.sb("ident", [P, P])
        top = m.sb("top", [P, B * TT])
        den = m.sb("den", [P, B * TT])
        inv = m.sb("inv", [P, B * TT])
        probs = m.sb("probs", [P, B, TT, NE])
        by_tile = m.sb("by_tile", [P, TT, B, NE])
        rows = m.sb("rows", [P, 2, S])
        work = m.sb("work", [P, 2, S])
        best = m.sb("best", [P, 2, 8])
        mask = m.sb("mask", [P, 2, S])
        ones = m.sb("ones", [P, S])
        order = m.sb("order", [P, 2, S])
        slot = m.sb("slot", [P, 2, S])
        tp = m.ps("tp", [P, 2, S])
        tb = m.ps("tb", [P, 2, S])
        const_in = m.sem("const_in")
        step = m.sem("step")
        exped = m.sem("exped")
        turned = m.sem("turned")
        row = m.sem("row")
        taken = [m.sem(f"taken{h}") for h in range(2)]
        slotted = m.sem("slotted")
        back = m.sem("back")
        stored = m.sem("stored")
        g3 = gate[:, :, :, :].rearrange("p b t e -> p (b t) e")
        p3 = probs[:, :, :, :].rearrange("p b t e -> p (b t) e")

        with nc.Block() as block:

            @block.sync
            def _(sp):
                sp.dma_start(ident[:, :], ident_d).then_inc(const_in, 16)
                wait_alone(sp, row, 2)
                sp.dma_start(prob_d.rearrange("(h r) t -> r h t", h=2), rows[:, :, :]).then_inc(stored, 16)
                wait_alone(sp, slotted, 2)
                sp.dma_start(slot_d.rearrange("(h r) t -> r h t", h=2), slot[:, :, :]).then_inc(stored, 16)
                wait_alone(sp, stored, 32)

            @block.vector
            def _(dve):
                dve.memset(ones[:, :], 1.0)
                dve.tensor_reduce(top[:, :], g3, AX_X, ALU.max).then_inc(step, 1)
                dve.wait_ge(step, 1)
                spread = top[:, :].unsqueeze(2).to_broadcast([P, B * TT, NE])
                dve.tensor_tensor(p3, g3, spread, ALU.subtract).then_inc(step, 1)
                dve.wait_ge(exped, 1)
                dve.tensor_reduce(den[:, :], p3, AX_X, ALU.add).then_inc(step, 1)
                dve.wait_ge(step, 3)
                dve.reciprocal(inv[:, :], den[:, :]).then_inc(step, 1)
                dve.wait_ge(step, 4)
                dve.tensor_tensor(by_tile[:, :, :, :].rearrange("p t b e -> p b t e"), probs[:, :, :, :],
                                  inv[:, :].rearrange("p (b t) -> p b t", t=TT).unsqueeze(3).to_broadcast([P, B, TT, NE]),
                                  ALU.mult).then_inc(step, 1)
                dve.wait_ge(turned, 1)
                for h in range(2):
                    dve.tensor_copy(rows[:, h], tp[:, h]).then_inc(row, 1)
                dve.wait_ge(row, 2)
                for k in range(CAP // 8):
                    for h in range(2):
                        src = rows if k == 0 else work
                        if k:
                            dve.wait_ge(taken[h], 2 * k)
                        dve.max(best[:, h], src[:, h]).then_inc(taken[h], 1)
                    for h in range(2):
                        src = rows if k == 0 else work
                        dve.wait_ge(taken[h], 2 * k + 1)
                        dve.match_replace(work[:, h], best[:, h], src[:, h], -1.0).then_inc(taken[h], 1)
                for h in range(2):
                    dve.wait_ge(taken[h], 2 * (CAP // 8))
                    dve.tensor_scalar(mask[:, h], work[:, h], 0.0, None, ALU.is_lt).then_inc(taken[h], 1)
                    dve.wait_ge(taken[h], 2 * (CAP // 8) + 1)
                    dve.tensor_tensor_scan(order[:, h], ones[:, :], mask[:, h], 0.0, ALU.mult, ALU.add).then_inc(taken[h], 1)
                    dve.wait_ge(taken[h], 2 * (CAP // 8) + 2)
                    dve.tensor_tensor(order[:, h], order[:, h], mask[:, h], ALU.mult).then_inc(taken[h], 1)
                    dve.wait_ge(taken[h], 2 * (CAP // 8) + 3)
                    dve.tensor_scalar(slot[:, h], order[:, h], -1.0, None, ALU.add).then_inc(slotted, 1)
                dve.wait_ge(back, 1)
                for h in range(2):
                    dve.tensor_copy(slot_t[:, h * HALF:(h + 1) * HALF].rearrange("p b t e -> p t b e"),
                                    tb[:, h].rearrange("p (t b e) -> p t b e", t=TT, e=NE))

            @block.scalar
            def _(act):
                act.wait_ge(step, 2)
                act.activation(p3, p3, ACT.Exp).then_inc(exped, 1)

            @block.tensor
            def _(pe):
                pe.wait_ge(const_in, 16)
                pe.wait_ge(step, 5)
                for h in range(2):
                    for t in range(TT):
                        ins = pe.transpose(tp[:, h, t * P:(t + 1) * P],
                                           by_tile[:, t, h * HALF:(h + 1) * HALF, :].rearrange("p b e -> p (b e)"), ident[:, :])
                ins.then_inc(turned, 1)
                pe.wait_ge(slotted, 2)
                for h in range(2):
                    for t in range(TT):
                        ins = pe.transpose(tb[:, h, t * P:(t + 1) * P], slot[:, h, t * P:(t + 1) * P], ident[:, :])
                ins.then_inc(back, 1)


def gather_phase(nc, slots_d, slot_t, xn_d, xin_d):
    with ExitStack() as ctx:
        m = Memory(nc, ctx, "gather")
        slots = m.sb("slots", [P, CAP])
        xn = m.sb("xn", [P, 2, TT, D])
        xs = m.sb("xs", [P, 2, 2, TT, D], F32R)
        pick = m.sb("pick", [P, 2, TT, NE, CAP], F32R)
        out = m.sb("out", [P, 2, DC, NE, CAP])
        gp = m.ps("gp", [P, 4, S])
        const_in = m.sem("const_in")
        x_in = [m.sem(f"x_in{s}") for s in range(2)]
        high = m.sem("high")
        low = m.sem("low")
        picked = m.sem("picked")
        gathered = m.sem("gathered")
        out_a = m.sem("out_a")
        out_b = m.sem("out_b")
        stored = [m.sem(f"stored{s}") for s in range(2)]

        def compare(eng, t, s, b):
            return eng.tensor_tensor(pick[:, s, t],
                                     slots[:, :].unsqueeze(1).to_broadcast([P, NE, CAP]),
                                     slot_t[:, bass.ds(b, 1), t, :].rearrange("p o e -> p (o e)").unsqueeze(2).to_broadcast([P, NE, CAP]),
                                     ALU.is_equal)

        with nc.Block() as block:

            @block.sync
            def _(sp):
                sp.dma_start(slots[:, :], slots_d).then_inc(const_in, 16)

                def body(i):
                    for s in range(2):
                        b = i * 2 + s
                        wait_alone(sp, low, b - 1)
                        sp.dma_start(xn[:, s], xn_d[bass.ds(b, 1)].rearrange("o p t d -> p (o t) d")).then_inc(x_in[s], 16)

                first_apart(sp, B // 2, body)

            @block.gpsimd
            def _(pool):
                def body(i):
                    for s in range(2):
                        b = i * 2 + s
                        wait_alone(pool, out_a, (b + 1) * 2)
                        wait_alone(pool, out_b, (b + 1) * 2)
                        for c in range(DC):
                            pool.dma_start(xin_d[:, bass.ds(b, 1), :, c].rearrange("e o p k -> p (o e) k"), out[:, s, c]).then_inc(stored[s], 16)

                first_apart(pool, B // 2, body)
                for s in range(2):
                    wait_alone(pool, stored[s], 32 * (B // 2))

            @block.vector
            def _(dve):
                dve.wait_ge(const_in, 16)

                def body(i):
                    for s in range(2):
                        b = i * 2 + s
                        wait(dve, gathered, (b - 1) * 4)
                        for t in range(TT):
                            compare(dve, t, s, b).then_inc(picked, 1)
                        dve.wait_ge(high, b + 1)
                        dve.tensor_tensor(xs[:, s, 1], xn[:, s], xs[:, s, 0].bitcast(F32), ALU.subtract).then_inc(low, 1)
                        wait(dve, stored[s], i * 32)
                        for k in (0, 2):
                            dve.wait_ge(gathered, b * 4 + k + 1)
                            c, q = k // 2, k % 2
                            dve.tensor_copy(out[:, s, c, q * 4:(q + 1) * 4], gp[:, k].rearrange("p (e k) -> p e k", e=4)).then_inc(out_a, 1)

                first_apart(dve, B // 2, body)

            @block.scalar
            def _(act):
                def body(i):
                    for s in range(2):
                        b = i * 2 + s
                        act.wait_ge(x_in[s], (i + 1) * 16)
                        wait(act, gathered, (b - 1) * 4)
                        act.activation(xs[:, s, 0], xn[:, s], ACT.Copy).then_inc(high, 1)
                        wait(act, stored[s], i * 32)
                        for k in (1, 3):
                            act.wait_ge(gathered, b * 4 + k + 1)
                            c, q = k // 2, k % 2
                            act.activation(out[:, s, c, q * 4:(q + 1) * 4], gp[:, k].rearrange("p (e k) -> p e k", e=4),
                                           ACT.Copy).then_inc(out_b, 1)

                first_apart(act, B // 2, body)

            @block.tensor
            def _(pe):
                def body(i):
                    for s in range(2):
                        b = i * 2 + s
                        pe.wait_ge(picked, (b + 1) * TT)
                        pe.wait_ge(low, b + 1)
                        for k in range(4):
                            c, q = k // 2, k % 2
                            wait(pe, (out_a, out_b)[k % 2], (b - 1) * 2 + k // 2 + 1)
                            for t in range(TT):
                                for a in range(2):
                                    ins = pe.matmul(gp[:, k], xs[:, s, a, t, c * P:(c + 1) * P],
                                                    pick[:, s, t, q * 4:(q + 1) * 4, :],
                                                    start=(t == 0 and a == 0), stop=(t == TT - 1 and a == 1))
                            ins.then_inc(gathered, 1)

                first_apart(pe, B // 2, body)


def attention_phase(nc, w, consts, xt_d, xs_d, att_d):
    sin_d, ident_d, spread_d, keep_d = consts
    LEAD = 3
    LAG = 2
    NX = 4
    HEADS = B * H
    UNITS = B * NQ
    with ExitStack() as ctx:
        m = Memory(nc, ctx, "att")
        ident = m.sb("ident", [P, P])
        spread = m.sb("spread", [P, P])
        keep = m.sb("keep", [P, QH])
        bias_u = m.sb("bias_u", [P, NQ])
        bias_v = m.sb("bias_v", [P, NQ])
        bias_k = m.sb("bias_k", [P, NQ])
        bias_p = m.sb("bias_p", [P, NQ])
        raw = m.sb("raw", [P, 3, NQ])
        bv = m.sb("bv", [P, D])
        wq = m.sb("wq", [P, 2, DC, NQ, P], F32R)
        wk = m.sb("wk", [P, 2, DC, NQ, P], F32R)
        wv = m.sb("wv", [P, 2, DC, D], F32R)
        pos = m.sb("pos", [P, 2, NQ, S], F32R)
        shared = m.sb("shared", [P, 4, TT, S])
        shifted = m.sb("shifted", [P, NX, TT, S])
        wst = shared[:, 0:3, :, :].rearrange("p k t s -> p k (t s)")
        sinus = shifted[:, 0].rearrange("p t s -> p (t s)")[:, 0:DC * S].rearrange("p (c s) -> p c s", c=DC)
        wpd = shifted[:, 1].rearrange("p t s -> p (t s)")[:, 0:DC * NQ * P].rearrange("p (c q n) -> p c q n", c=DC, q=NQ)

        xt = m.sb("xt", [P, 2, DC, S], F32R)
        qd = m.sb("qd", [P, 2, 2, S], F32R)
        kd = m.sb("kd", [P, 2, 2, S], F32R)
        qu = m.sb("qu", [P, QH, S], F32R)
        qv = m.sb("qv", [P, QH, S], F32R)
        vst = m.sb("vst", [P, TT, D])
        val = m.sb("val", [P, TT, H, 32])
        xo = m.sb("xo", [P, 2, TT, S + 1])
        mx = m.sb("mx", [P, 4, TT])
        nm = m.sb("nm", [P, 4, TT])
        pt = m.sb("pt", [P, 2, TT, S])
        osb = m.sb("osb", [P, 2, S])
        inv = m.sb("inv", [P, S])
        on = m.sb("on", [P, 2, QH, P])

        xp = m.ps("xp", [P, 2, S])
        sp_ = m.ps("sp", [P, 2, S])
        tp = m.ps("tp", [P, 2, S])
        op = m.ps("op", [P, S])
        mp = m.ps("mp", [P, S])

        const_in = m.sem("const_in")
        set_up = m.sem("set_up")
        set_hi = m.sem("set_hi")
        p_full = m.sem("p_full")
        p_hi = m.sem("p_hi")
        p_lo = m.sem("p_lo")
        ones_set = m.sem("ones_set")
        edge_set = m.sem("edge_set")
        xt_in = m.sem("xt_in")
        q_full = m.sem("q_full")
        q_high = m.sem("q_high")
        q_low = m.sem("q_low")
        k_full = m.sem("k_full")
        k_high = m.sem("k_high")
        k_low = m.sem("k_low")
        v_full = m.sem("v_full")
        v_staged = m.sem("v_staged")
        v_ready = m.sem("v_ready")
        qv_ready = m.sem("qv_ready")
        qu_ready = m.sem("qu_ready")
        x_full = m.sem("x_full")
        x_out = m.sem("x_out")
        x_written = [m.sem(f"x_written{k}") for k in range(NX)]
        x_shifted = [m.sem(f"x_shifted{k}") for k in range(NX)]
        s_full = m.sem("s_full")
        added = m.sem("added")
        max_ready = m.sem("max_ready")
        exp_done = m.sem("exp_done")
        t_full = m.sem("t_full")
        t_out = m.sem("t_out")
        o_full = m.sem("o_full")
        o_out = m.sem("o_out")
        r_full = m.sem("r_full")
        r_out = m.sem("r_out")
        o_scaled = m.sem("o_scaled")
        o_stored = [m.sem(f"o_stored{k}") for k in range(2)]

        def doubled(weight):
            return weight.rearrange("(c p) (q n) -> p c q n", p=P, q=NQ)

        def columns(vector):
            return vector.rearrange("(q n) -> n q", q=NQ)

        with nc.Block() as block:

            @block.sync
            def _(sp):
                sp.dma_start(ident[:, :], ident_d).then_inc(const_in, 16)
                sp.dma_start(spread[:, :], spread_d).then_inc(const_in, 16)
                sp.dma_start(keep[:, :], keep_d).then_inc(const_in, 16)
                sp.dma_start(sinus, sin_d.rearrange("(c p) t -> p c t", p=P)).then_inc(const_in, 16)
                for half in range(2):
                    rows = slice(64 * half, 64 * half + 64)
                    for c in range(DC):
                        at = slice(c * P, (c + 1) * P)
                        for dst, name in ((wst[:, 0], "Wq"), (wst[:, 1], "Wk")):
                            to = dst[:, 0:DC * NQ * P].rearrange("p (c q n) -> p c q n", c=DC, q=NQ)
                            sp.dma_start(to[:, c, :, rows], w[name][at].rearrange("p (q n) -> p q n", q=NQ)).then_inc(const_in, 16)
                        sp.dma_start(wpd[:, c, :, rows], w["Wp"][at].rearrange("p (q n) -> p q n", q=NQ)).then_inc(const_in, 16)
                    sp.dma_start(raw[rows, 0], columns(w["bq"]), allow_slow_non_contiguous=True).then_inc(const_in, 16)
                    sp.dma_start(raw[rows, 1], columns(w["u"]), allow_slow_non_contiguous=True).then_inc(const_in, 16)
                    sp.dma_start(raw[rows, 2], columns(w["v"]), allow_slow_non_contiguous=True).then_inc(const_in, 16)
                    sp.dma_start(bias_k[rows], columns(w["bk"]), allow_slow_non_contiguous=True).then_inc(const_in, 16)
                    sp.dma_start(bias_p[rows], columns(w["bp"]), allow_slow_non_contiguous=True).then_inc(const_in, 16)
                sp.dma_start(wst[:, 2, 0:DC * D].rearrange("p (c n) -> p c n", c=DC),
                             w["Wv"].rearrange("(c p) n -> p c n", p=P)).then_inc(const_in, 16)
                sp.dma_start(bv[:, :], w["bv"].partition_broadcast(P)).then_inc(const_in, 16)

                def load_xt(b):
                    sp.dma_start(xt[:, :, :, :].bitcast(F32), xt_d[bass.ds(b, 1)].rearrange("o p k c t -> p (o k) c t")).then_inc(xt_in, 16)

                def write_x(b, k):
                    slot, turn = k % NX, b * NQ + k // NX
                    wait_alone(sp, x_out, (b * H + k) * 2 + 2)
                    wait_alone(sp, x_shifted[slot], turn * 16)
                    sp.dma_start(xs_d[slot].rearrange("(t p c) -> p t c", t=TT, c=S + 1), xo[:, k % 2]).then_inc(x_written[slot], 16)

                def read_x(b, k):
                    slot, turn = k % NX, b * NQ + k // NX
                    wait_alone(sp, x_written[slot], (turn + 1) * 16)
                    wait_alone(sp, added, (b * H + k - NX + 1) * TT)
                    sp.dma_start(shifted[:, slot], xs_d[slot][S:S + S * S].rearrange("(t p c) -> p t c", t=TT, c=S)).then_inc(x_shifted[slot], 16)

                def store_o(b, q):
                    u = b * NQ + q
                    wait_alone(sp, o_scaled, u + 1)
                    for t in range(TT):
                        dst = att_d[bass.ds(b + q // NQ, 1)].rearrange("o (q h v) t -> (o q) v h t", q=NQ, h=QH)
                        sp.dma_start(dst[q % NQ, :, :, t * P:(t + 1) * P], on[32 * t:32 * t + HD, q % 2]).then_inc(o_stored[q % 2], 16)

                load_xt(0)
                wait_alone(sp, p_lo, NQ)
                wait_alone(sp, set_up, 4)
                write_x(0, 0)
                write_x(0, 1)
                read_x(0, 0)
                write_x(0, 2)
                read_x(0, 1)

                def body(b):
                    first = isinstance(b, int) and b == 0
                    last = isinstance(b, int) and b == B - 1
                    for k in range(H):
                        if not (last and k + LEAD >= H):
                            write_x(b, k + LEAD)
                        if not (last and k + LEAD - 1 >= H):
                            read_x(b, k + LEAD - 1)
                        if k % QH == 0 and not (first and k < 2 * QH):
                            store_o(b, k // QH - 2)
                        if k == 2 * QH + 1 and not last:
                            wait_alone(sp, k_full, b * NQ + NQ)
                            load_xt(b + 1)

                ends_apart(sp, B, body)
                store_o(B - 1, NQ - 2)
                store_o(B - 1, NQ - 1)
                for k in range(2):
                    wait_alone(sp, o_stored[k], UNITS // 2 * TT * 16)

            @block.gpsimd
            def _(pool):
                pool.memset(val[:, :, :, :], 0.0).then_inc(ones_set, 1)
                wait_alone(pool, ones_set, 1)
                pool.memset(val[:, :, :, HD:HD + 1], 1.0).then_inc(ones_set, 1)
                pool.memset(xo[:, :, :, 0:1], 0.0).then_inc(edge_set, 1)
                wait_alone(pool, const_in, 16 * CONST_LOADS)

                def keep_head(dst, src, h):
                    return pool.tensor_scalar(dst[:, h], src.bitcast(F32), keep[:, h:h + 1], None, ALU.mult)

                def heads_v(b, q):
                    u = b * NQ + q
                    wait_alone(pool, q_low, u * 2 + 2)
                    for h in range(QH):
                        wait_alone(pool, x_full, ((u - 1) * QH + h + 1) * 2)
                        keep_head(qv, qd[:, q % 2, 1], h).then_inc(qv_ready, 1)

                def head_u(b, q, h):
                    u = b * NQ + q
                    wait_alone(pool, s_full, ((u - 1) * QH + h + 1) * TT)
                    keep_head(qu, qd[:, q % 2, 0], h).then_inc(qu_ready, 1)

                def values(b):
                    wait_alone(pool, v_staged, b * 2 + 2)
                    wait_alone(pool, o_full, b * H)
                    pool.tensor_copy(val[:, :, :, 0:HD], vst[:, :, :].rearrange("p t (h v) -> p t h v", h=H)).then_inc(v_ready, 1)

                def scale_o(b, q):
                    u = b * NQ + q
                    wait_alone(pool, r_out, u + 1)
                    wait_alone(pool, o_stored[q % 2], (u - q % 2) * (TT * 8))
                    pool.tensor_tensor(on[:, q % 2], osb[:, q % 2].rearrange("p (h t) -> p h t", h=QH),
                                       inv[:, :].rearrange("p (h t) -> p h t", h=QH), ALU.mult).then_inc(o_scaled, 1)

                wait_alone(pool, ones_set, 2)
                heads_v(0, 0)
                for h in range(QH):
                    head_u(0, 0, h)

                def body(b):
                    first = isinstance(b, int) and b == 0
                    last = isinstance(b, int) and b == B - 1
                    for q in range(NQ):
                        ahead = not (last and q == NQ - 1)
                        if ahead:
                            heads_v(b, q + 1)
                            head_u(b, q + 1, 0)
                        if q == 0:
                            values(b)
                        if ahead:
                            for h in range(1, QH):
                                head_u(b, q + 1, h)
                        if not (first and q == 0):
                            scale_o(b, q - 1)

                ends_apart(pool, B, body)
                scale_o(B - 1, NQ - 1)

            @block.scalar
            def _(act):
                act.wait_ge(const_in, 16 * CONST_LOADS)
                act.activation(wq[:, 0].rearrange("p c q n -> p (c q n)"), wst[:, 0, 0:DC * NQ * P], ACT.Copy).then_inc(set_hi, 1)
                act.activation(wk[:, 0].rearrange("p c q n -> p (c q n)"), wst[:, 1, 0:DC * NQ * P], ACT.Copy).then_inc(set_hi, 1)
                act.activation(wv[:, 0].rearrange("p c n -> p (c n)"), wst[:, 2, 0:DC * D], ACT.Copy).then_inc(set_hi, 1)
                for q in range(NQ):
                    act.wait_ge(p_full, q + 1)
                    act.activation(pos[:, 0, q], mp[:, :], ACT.Identity, bias=bias_p[:, q:q + 1]).then_inc(p_hi, 1)

                def q_highs(b, q):
                    u = b * NQ + q
                    act.wait_ge(q_full, u + 1)
                    wait(act, qu_ready, (u - 1) * QH)
                    act.activation(qd[:, q % 2, 0], mp[:, :], ACT.Identity, bias=bias_u[:, q % NQ:q % NQ + 1]).then_inc(q_high, 1)
                    act.activation(qd[:, q % 2, 1], mp[:, :], ACT.Identity, bias=bias_v[:, q % NQ:q % NQ + 1]).then_inc(q_high, 1)

                def k_highs(b, q):
                    u = b * NQ + q
                    act.wait_ge(k_full, u + 1)
                    wait(act, s_full, (u - 1) * QH * TT)
                    act.activation(kd[:, q % 2, 0], mp[:, :], ACT.Identity, bias=bias_k[:, q % NQ:q % NQ + 1]).then_inc(k_high, 1)

                def x_evacuate(b, k):
                    n = b * H + k
                    if not (isinstance(b, int) and b * H + k < 2):
                        act.wait_ge(x_written[(k - 2) % NX], (b * NQ + (k - 2) // NX + 1) * 16)
                    for half in range(2):
                        act.wait_ge(x_full, n * 2 + half + 1)
                        act.activation(xo[:, k % 2, 2 * half:2 * half + 2, 1:S + 1], xp[:, :, :], ACT.Copy).then_inc(x_out, 1)

                def o_evacuate(b, q):
                    u = b * NQ + q
                    act.wait_ge(o_full, (u + 1) * QH)
                    wait(act, o_scaled, u - 1)
                    act.activation(osb[:, q % 2], op[:, :], ACT.Copy).then_inc(o_out, 1)

                act.wait_ge(set_up, 2)
                act.wait_ge(edge_set, 1)
                q_highs(0, 0)
                k_highs(0, 0)
                for k in range(LEAD):
                    x_evacuate(0, k)

                def body(b):
                    first = isinstance(b, int) and b == 0
                    last = isinstance(b, int) and b == B - 1
                    for k in range(H):
                        q, hh = k // QH, k % QH
                        n = b * H + k
                        ahead = not (last and q == NQ - 1)
                        if hh == 0 and ahead:
                            q_highs(b, q + 1)
                        if hh == 1 and ahead:
                            k_highs(b, q + 1)
                        if hh == 2 and not (first and q == 0):
                            o_evacuate(b, q - 1)
                        if not (last and k + LEAD >= H):
                            x_evacuate(b, k + LEAD)
                        for t in range(TT):
                            act.wait_ge(max_ready, n + 1)
                            act.activation(shared[:, k % 4, t], shared[:, k % 4, t], ACT.Exp, bias=nm[:, k % 4, t:t + 1],
                                           scale=0.25).then_inc(exp_done, 1)

                ends_apart(act, B, body)
                o_evacuate(B - 1, NQ - 1)

            @block.vector
            def _(dve):
                dve.wait_ge(const_in, 16 * CONST_LOADS)
                dve.tensor_tensor(bias_u[:, :], raw[:, 0], raw[:, 1], ALU.add).then_inc(set_up, 1)
                dve.tensor_tensor(bias_v[:, :], raw[:, 0], raw[:, 2], ALU.add).then_inc(set_up, 1)
                dve.wait_ge(set_up, 2)
                dve.wait_ge(set_hi, 3)
                dve.tensor_tensor(wq[:, 1].rearrange("p c q n -> p (c q n)"), wst[:, 0, 0:DC * NQ * P],
                                  wq[:, 0].rearrange("p c q n -> p (c q n)").bitcast(F32), ALU.subtract)
                dve.tensor_tensor(wk[:, 1].rearrange("p c q n -> p (c q n)"), wst[:, 1, 0:DC * NQ * P],
                                  wk[:, 0].rearrange("p c q n -> p (c q n)").bitcast(F32), ALU.subtract).then_inc(set_up, 1)
                dve.tensor_tensor(wv[:, 1].rearrange("p c n -> p (c n)"), wst[:, 2, 0:DC * D],
                                  wv[:, 0].rearrange("p c n -> p (c n)").bitcast(F32), ALU.subtract).then_inc(set_up, 1)
                dve.wait_ge(set_up, 4)

                def less_high(out, psum, bias, rows=slice(0, P)):
                    high_part, low_part = out
                    return dve.scalar_tensor_tensor(low_part[rows], psum[rows], bias[rows], high_part[rows].bitcast(F32),
                                                    ALU.add, ALU.subtract)

                for q in range(NQ):
                    dve.wait_ge(p_hi, q + 1)
                    less_high((pos[:, 0, q], pos[:, 1, q]), mp, bias_p[:, q:q + 1]).then_inc(p_lo, 1)

                def q_lows(b, q):
                    u = b * NQ + q
                    dve.wait_ge(q_high, u * 2 + 2)
                    for k, bias in enumerate((bias_u, bias_v)):
                        less_high((qd[:, q % 2, k], qd[:, q % 2, k]), mp, bias[:, q % NQ:q % NQ + 1],
                                  slice(64, P)).then_inc(q_low, 1)

                def k_lows(b, q):
                    u = b * NQ + q
                    dve.wait_ge(k_high, u + 1)
                    less_high((kd[:, q % 2, 0], kd[:, q % 2, 1]), mp, bias_k[:, q % NQ:q % NQ + 1]).then_inc(k_low, 1)

                def stage_v(b, half):
                    dve.wait_ge(v_full, b * 2 + half + 1)
                    wait(dve, v_ready, b)
                    dve.tensor_tensor(vst[:, 2 * half:2 * half + 2], mp[:, :].rearrange("p (t n) -> p t n", t=2),
                                      bv[:, :].unsqueeze(1).to_broadcast([P, 2, D]), ALU.add).then_inc(v_staged, 1)

                def add(b, k, t):
                    n = b * H + k
                    if t == 0:
                        dve.wait_ge(x_shifted[k % NX], (b * NQ + k // NX + 1) * 16)
                        wait(dve, t_full, (n - 3) * TT)
                    wait_alone(dve, s_full, n * TT + t + 1)
                    dve.tensor_tensor_reduce(out=shared[:, k % 4, t], in0=sp_[:, t % 2], in1=shifted[:, k % NX, t], scale=1.0,
                                             scalar=NEG, op0=ALU.add, op1=ALU.max,
                                             accum_out=mx[:, k % 4, t:t + 1]).then_inc(added, 1)

                def t_evacuate(b, k, t):
                    n = b * H + k
                    dve.wait_ge(t_full, n * TT + t + 1)
                    if t == 0:
                        wait(dve, o_full, n - 1)
                    dve.tensor_copy(pt[:, k % 2, t], tp[:, t % 2]).then_inc(t_out, 1)

                def invert(b, q):
                    u = b * NQ + q
                    dve.wait_ge(r_full, u + 1)
                    wait(dve, o_scaled, u)
                    dve.reciprocal(inv[:, :], mp[:, :]).then_inc(r_out, 1)

                q_lows(0, 0)
                k_lows(0, 0)
                stage_v(0, 0)
                stage_v(0, 1)

                def body(b):
                    first = isinstance(b, int) and b == 0
                    last = isinstance(b, int) and b == B - 1
                    for k in range(H):
                        q, hh = k // QH, k % QH
                        n = b * H + k
                        ahead = not (last and q == NQ - 1)
                        for t in range(TT):
                            add(b, k, t)
                            if t == 0 and ahead:
                                if hh == 0:
                                    q_lows(b, q + 1)
                                if hh == 1:
                                    k_lows(b, q + 1)
                            if t == 0 and q == NQ - 1 and not last:
                                if hh == 2:
                                    stage_v(b + 1, 0)
                                if hh == 3:
                                    stage_v(b + 1, 1)
                            if t == TT - 1:
                                dve.wait_ge(added, n * TT + TT)
                                dve.tensor_scalar(nm[:, k % 4], mx[:, k % 4], -0.25, None, ALU.mult).then_inc(max_ready, 1)
                            if not (first and k < LAG):
                                t_evacuate(b, k - LAG, t)
                        if hh == 3 and not (first and q == 0):
                            invert(b, q - 1)

                ends_apart(dve, B, body)
                for k in range(LAG):
                    for t in range(TT):
                        t_evacuate(B, k - LAG, t)
                invert(B - 1, NQ - 1)

            @block.tensor
            def _(pe):
                pe.wait_ge(const_in, 16 * CONST_LOADS)
                for q in range(NQ):
                    wait(pe, p_lo, q)
                    for c in range(DC):
                        ins = pe.matmul(mp[:, :], wpd[:, c, q, :], sinus[:, c, :], start=(c == 0), stop=(c == DC - 1))
                    ins.then_inc(p_full, 1)
                pe.wait_ge(set_up, 4)
                pe.wait_ge(p_lo, NQ)

                def project(weight, q, sem):
                    for k, (wi, xi) in enumerate(SPLITS):
                        for c in range(DC):
                            ins = pe.matmul(mp[:, :], weight[:, wi, c, q % NQ, :], xt[:, xi, c, :],
                                            start=(k == 0 and c == 0), stop=(k == 2 and c == DC - 1))
                    ins.then_inc(sem, 1)

                def project_q(b, q):
                    u = b * NQ + q
                    pe.wait_ge(xt_in, (b + 1 + q // NQ) * 16)
                    wait(pe, k_low, u)
                    wait(pe, r_out, u - 2)
                    project(wq, q, q_full)

                def project_k(b, q):
                    u = b * NQ + q
                    pe.wait_ge(q_low, u * 2 + 2)
                    project(wk, q, k_full)

                def project_v(b, half):
                    pe.wait_ge(k_low, b * NQ + 1)
                    wait(pe, v_staged, b * 2 + half)
                    for t in range(2):
                        tok = (2 * half + t) * P
                        for k, (wi, xi) in enumerate(SPLITS):
                            for c in range(DC):
                                ins = pe.matmul(mp[:, t * D:(t + 1) * D], xt[:, xi, c, tok:tok + P], wv[:, wi, c, :],
                                                start=(k == 0 and c == 0), stop=(k == 2 and c == DC - 1))
                    ins.then_inc(v_full, 1)

                def position(b, k, half):
                    n = b * H + k
                    if half == 0:
                        pe.wait_ge(qv_ready, n + 1)
                    wait(pe, x_out, n * 2 + half)
                    for t in range(2):
                        tok = (2 * half + t) * P
                        for part in range(2):
                            ins = pe.matmul(xp[:, t, :], qv[:, k % QH, tok:tok + P], pos[:, part, k // QH % NQ, :],
                                            start=(part == 0), stop=(part == 1))
                    ins.then_inc(x_full, 1)

                def content(b, k, t):
                    n = b * H + k
                    if t == 0:
                        pe.wait_ge(qu_ready, n + 1)
                        pe.wait_ge(k_low, b * NQ + k // QH + 1)
                    wait(pe, added, n * TT + t - 1)
                    for part in range(2):
                        ins = pe.matmul(sp_[:, t % 2, :], qu[:, k % QH, t * P:(t + 1) * P], kd[:, k // QH % 2, part, :],
                                        start=(part == 0), stop=(part == 1))
                    ins.then_inc(s_full, 1)

                def turn(b, k, c):
                    n = b * H + k
                    pe.wait_ge(exp_done, (n + 1) * TT)
                    wait(pe, t_out, n * TT + c - 1)
                    for t in range(TT):
                        ins = pe.transpose(tp[:, c % 2, t * P:(t + 1) * P], shared[:, k % 4, t, c * P:(c + 1) * P], ident[:, :])
                    ins.then_inc(t_full, 1)

                def times_values(b, k):
                    n = b * H + k
                    pe.wait_ge(v_ready, b + (1 if k >= 0 else 0))
                    if k % QH == 0:
                        wait(pe, o_out, b * NQ + k // QH)
                    for c in range(TT):
                        pe.wait_ge(t_out, n * TT + c + 1)
                        for t in range(TT):
                            ins = pe.matmul(op[32 * t:32 * t + 32, k % QH * P:(k % QH + 1) * P], val[:, c, k % H, :],
                                            pt[:, k % 2, c, t * P:(t + 1) * P], start=(c == 0), stop=(c == TT - 1))
                    ins.then_inc(o_full, 1)

                def spread_sums(b, q, after_k, after_v):
                    u = b * NQ + q
                    pe.wait_ge(o_out, u + 1)
                    pe.wait_ge(k_low, after_k)
                    if after_v is not None:
                        pe.wait_ge(v_staged, after_v)
                    wait(pe, r_out, u)
                    pe.matmul(mp[:, :], spread[:, :], osb[:, q % 2, :], start=True, stop=True).then_inc(r_full, 1)

                project_q(0, 0)
                project_k(0, 0)
                project_v(0, 0)
                project_v(0, 1)
                pe.wait_ge(v_staged, 2)
                for k in range(LEAD):
                    position(0, k, 0)
                    position(0, k, 1)

                def body(b):
                    first = isinstance(b, int) and b == 0
                    last = isinstance(b, int) and b == B - 1
                    for k in range(H):
                        q, hh = k // QH, k % QH
                        ahead = not (last and q == NQ - 1)
                        if hh == 0 and ahead:
                            project_q(b, q + 1)
                        if hh == 1 and ahead:
                            project_k(b, q + 1)
                        if q == NQ - 1 and not last:
                            if hh == 2:
                                project_v(b + 1, 0)
                            if hh == 3:
                                project_v(b + 1, 1)
                        for t in range(TT):
                            content(b, k, t)
                            if t == 1 and hh == 3 and not (first and q == 0):
                                spread_sums(b, q - 1, b * NQ + q + (2 if ahead else 1),
                                            (b + 2) * 2 if q == NQ - 1 and not last else None)
                            if not (first and k < LAG):
                                turn(b, k - LAG, t)
                            if t % 2 and not (last and k + LEAD >= H):
                                position(b, k + LEAD, t // 2)
                        if not (first and k < LAG):
                            times_values(b, k - LAG)

                ends_apart(pe, B, body)
                for k in range(LAG):
                    for t in range(TT):
                        turn(B, k - LAG, t)
                    times_values(B, k - LAG)
                spread_sums(B - 1, NQ - 1, UNITS, None)


CONST_LOADS = 4 + 2 * (3 * DC + 5) + 2


def ffn_phase(nc, w1, w2, xin_d, y_d):
    with ExitStack() as ctx:
        m = Memory(nc, ctx, "ffn")
        w1s = m.sb("w1s", [P, DC, F])
        w2s = m.sb("w2s", [P, FC, D])
        w1p = m.sb("w1p", [P, 2, DC, F], F32R)
        w2p = m.sb("w2p", [P, 2, FC, D], F32R)
        xf = m.sb("xf", [P, 2, DC, GB, CAP])
        xp = m.sb("xp", [P, 2, 2, DC, GB * CAP], F32R)
        hf = m.sb("hf", [P, 2, S])
        hp = m.sb("hp", [P, 2, 2, FC, S], F32R)
        ys = m.sb("ys", [P, 2, GB, D])
        up = m.ps("up", [P, 4, S])
        yp = m.ps("yp", [P, 2, S])
        w1_in = m.sem("w1_in")
        w2_in = m.sem("w2_in")
        w1_high = m.sem("w1_high")
        w1_low = m.sem("w1_low")
        w2_high = m.sem("w2_high")
        w2_low = m.sem("w2_low")
        x_in = [m.sem(f"x_in{s}") for s in range(2)]
        x_high = m.sem("x_high")
        x_low = m.sem("x_low")
        up_full = m.sem("up_full")
        h_high = m.sem("h_high")
        h_full = m.sem("h_full")
        h_low = m.sem("h_low")
        y_full = m.sem("y_full")
        y_out = m.sem("y_out")
        y_stored = [m.sem(f"y_stored{s}") for s in range(2)]

        with nc.Block() as block:

            @block.sync
            def _(sp):
                def load_w(e):
                    wait_alone(sp, w1_low, e)
                    sp.dma_start(w1s[:, :, :], w1[bass.ds(e, 1)].rearrange("o (c p) f -> p (o c) f", p=P)).then_inc(w1_in, 16)
                    wait_alone(sp, w2_low, e)
                    sp.dma_start(w2s[:, :, :], w2[bass.ds(e, 1)].rearrange("o (c p) d -> p (o c) d", p=P)).then_inc(w2_in, 16)

                def load_x(e, g):
                    t = e * NG + g
                    wait_alone(sp, x_low, t - 1)
                    for c in range(DC):
                        sp.dma_start(xf[:, g % 2, c], xin_d[bass.ds(e, 1), g * GB:(g + 1) * GB, :, c].rearrange("o b p k -> p (o b) k")
                                     ).then_inc(x_in[g % 2], 16)

                def body(e):
                    last = isinstance(e, int) and e == NE - 1
                    for g in range(NG):
                        load_x(e, g)
                        if g == 4 and not last:
                            load_w(e + 1)

                load_w(0)
                ends_apart(sp, NE, body)

            @block.gpsimd
            def _(pool):
                def body(e):
                    for g in range(NG):
                        t = e * NG + g
                        wait_alone(pool, y_out, (t + 1) * GB)
                        pool.dma_start(y_d[g * GB:(g + 1) * GB, :, bass.ds(e, 1), :].rearrange("b p o d -> p (b o) d"),
                                       ys[:, g % 2]).then_inc(y_stored[g % 2], 16)

                ends_apart(pool, NE, body)
                for s in range(2):
                    wait_alone(pool, y_stored[s], NE * NG // 2 * 16)

            @block.scalar
            def _(act):
                def split_w(stage, parts, arrived, done, used, e, when):
                    act.wait_ge(arrived, (e + 1) * 16)
                    wait(act, used, when)
                    act.activation(parts[:, 0], stage[:, :, :], ACT.Copy).then_inc(done, 1)

                def split_x(e, g):
                    t = e * NG + g
                    act.wait_ge(x_in[g % 2], (e * (NG // 2) + g // 2 + 1) * 32)
                    wait(act, up_full, (t - 1) * FC)
                    act.activation(xp[:, g % 2, 0], xf[:, g % 2].rearrange("p c b k -> p c (b k)"), ACT.Copy).then_inc(x_high, 1)

                def body(e):
                    last = isinstance(e, int) and e == NE - 1
                    split_w(w1s, w1p, w1_in, w1_high, up_full, e, e * (NG * FC))
                    for g in range(NG):
                        t = e * NG + g
                        for f in range(FC):
                            act.wait_ge(up_full, t * FC + f + 1)
                            if f == 0:
                                wait(act, y_full, (t - 1) * GB)
                            act.activation(hp[:, g % 2, 0, f], up[:, f % 4], ACT.Gelu_apprx_tanh).then_inc(h_high, 1)
                            wait(act, h_low, t * FC + f - 1)
                            act.activation(hf[:, f % 2], up[:, f % 4], ACT.Gelu_apprx_tanh).then_inc(h_full, 1)
                            if f == 2 and not (last and g == NG - 1):
                                split_x(e, g + 1)
                        if g == 0:
                            split_w(w2s, w2p, w2_in, w2_high, y_full, e, e * (NG * GB))

                split_x(0, 0)
                ends_apart(act, NE, body)

            @block.vector
            def _(dve):
                def split_x(e, g):
                    t = e * NG + g
                    dve.wait_ge(x_high, t + 1)
                    dve.tensor_tensor(xp[:, g % 2, 1], xf[:, g % 2].rearrange("p c b k -> p c (b k)"),
                                      xp[:, g % 2, 0].bitcast(F32), ALU.subtract).then_inc(x_low, 1)

                def y_evacuate(e, g, k):
                    t = e * NG + g
                    dve.wait_ge(y_full, t * GB + k + 1)
                    if k == 0:
                        wait(dve, y_stored[g % 2], (e * (NG // 2) + g // 2) * 16)
                    dve.tensor_copy(ys[:, g % 2, k], yp[:, k % 2, 0:D]).then_inc(y_out, 1)

                def body(e):
                    first = isinstance(e, int) and e == 0
                    last = isinstance(e, int) and e == NE - 1
                    dve.wait_ge(w1_high, e + 1)
                    dve.tensor_tensor(w1p[:, 1], w1s[:, :, :], w1p[:, 0].bitcast(F32), ALU.subtract).then_inc(w1_low, 1)
                    for g in range(NG):
                        t = e * NG + g
                        for f in range(FC):
                            dve.wait_ge(h_full, t * FC + f + 1)
                            dve.tensor_tensor(hp[:, g % 2, 1, f], hf[:, f % 2], hp[:, g % 2, 0, f].bitcast(F32),
                                              ALU.subtract).then_inc(h_low, 1)
                            if f == 2 and not (last and g == NG - 1):
                                split_x(e, g + 1)
                            if f % 2 and not (first and g == 0):
                                y_evacuate(e, g - 1, f // 2)
                        if g == 0:
                            dve.wait_ge(w2_high, e + 1)
                            dve.tensor_tensor(w2p[:, 1], w2s[:, :, :], w2p[:, 0].bitcast(F32), ALU.subtract).then_inc(w2_low, 1)

                split_x(0, 0)
                ends_apart(dve, NE, body)
                for k in range(GB):
                    y_evacuate(NE, -1, k)

            @block.tensor
            def _(pe):
                def down(e, g, k, half):
                    t = e * NG + g
                    if half == 0:
                        if k == 0:
                            pe.wait_ge(h_low, (t + 1) * FC)
                            pe.wait_ge(w2_low, e + (1 if g >= 0 else 0))
                        wait(pe, y_out, t * GB + k - 1)
                    for f in range(4 * half, 4 * half + 4):
                        for s, (hi, wi) in enumerate(SPLITS):
                            ins = pe.matmul(yp[:, k % 2, 0:D], hp[:, g % 2, hi, f, k * CAP:(k + 1) * CAP], w2p[:, wi, f, :],
                                            start=(f == 0 and s == 0), stop=(f == FC - 1 and s == 2))
                    if half == 1:
                        ins.then_inc(y_full, 1)

                def body(e):
                    first = isinstance(e, int) and e == 0
                    pe.wait_ge(w1_low, e + 1)
                    for g in range(NG):
                        t = e * NG + g
                        pe.wait_ge(x_low, t + 1)
                        for f in range(FC):
                            wait(pe, h_full, t * FC + f - 3)
                            for s, (wi, xi) in enumerate(SPLITS):
                                for c in range(DC):
                                    ins = pe.matmul(up[:, f % 4, :], w1p[:, wi, c, f * P:(f + 1) * P], xp[:, g % 2, xi, c, :],
                                                    start=(s == 0 and c == 0), stop=(s == 2 and c == DC - 1))
                            ins.then_inc(up_full, 1)
                            if not (first and g == 0):
                                down(e, g - 1, f // 2, f % 2)

                ends_apart(pe, NE, body)
                for k in range(GB):
                    down(NE, -1, k, 0)
                    down(NE, -1, k, 1)


def combine_phase(nc, x, Wo, bo, slot_col_d, slot_d, prob_d, y_d, att_d, out):
    with ExitStack() as ctx:
        m = Memory(nc, ctx, "out")
        wo = m.sb("wo", [P, DC, D])
        bob = m.sb("bob", [P, D])
        slot_col = m.sb("slot_col", [P, 1])
        srow = m.sb("srow", [P, 2, NE, S])
        prow = m.sb("prow", [P, 2, NE, S])
        back = m.sb("back", [P, 1, NE, S])
        y = m.sb("y", [P, 2, NE, D])
        att = m.sb("att", [P, 2, DC, S])
        xi = m.sb("xi", [P, 2, TT, D])
        xb = m.sb("xb", [P, 2, TT, D])
        ffn = m.sb("ffn", [P, 2, TT, D], BF16)
        res = m.sb("res", [P, 2, TT, D])
        ap = m.ps("ap", [P, 2, 2, D])
        fp = m.ps("fp", [P, 4, 2, D])
        const_in = m.sem("const_in")
        rows_in = [m.sem(f"rows_in{s}") for s in range(2)]
        b_in = [m.sem(f"b_in{s}") for s in range(2)]
        placed = m.sem("placed")
        a_full = m.sem("a_full")
        f_full = m.sem("f_full")
        a_out = m.sem("a_out")
        f_out = m.sem("f_out")
        biased = m.sem("biased")
        summed = m.sem("summed")
        stored = [m.sem(f"stored{s}") for s in range(2)]

        with nc.Block() as block:

            @block.sync
            def _(sp):
                sp.dma_start(wo[:, :, :], Wo.rearrange("(c p) n -> p c n", p=P)).then_inc(const_in, 16)
                sp.dma_start(bob[:, :], bo.partition_broadcast(P)).then_inc(const_in, 16)
                sp.dma_start(slot_col[:, :], slot_col_d).then_inc(const_in, 16)

                def body(i):
                    for s in range(2):
                        b = i * 2 + s
                        wait_alone(sp, placed, (b - 1) * NE)
                        for src, dst in ((slot_d, srow), (prob_d, prow)):
                            sp.dma_start(dst[:, s], src[bass.ds(b * NE, NE)].rearrange("e t -> (e t)").partition_broadcast(P)
                                         .rearrange("p (e t) -> p e t", e=NE)).then_inc(rows_in[s], 16)
                        wait_alone(sp, f_full, (b - 1) * 2)
                        wait_alone(sp, summed, (b - 1) * 2)
                        sp.dma_start(y[:, s], y_d[bass.ds(b, 1)].rearrange("o p e d -> p (o e) d")).then_inc(b_in[s], 16)
                        sp.dma_start(att[:, s], att_d[bass.ds(b, 1)].rearrange("o (c p) t -> p (o c) t", p=P)).then_inc(b_in[s], 16)
                        sp.dma_start(xi[:, s], x[bass.ds(b, 1)].rearrange("o (t p) d -> p (o t) d", p=P)).then_inc(b_in[s], 16)

                first_apart(sp, B // 2, body)

            @block.gpsimd
            def _(pool):
                wait_alone(pool, const_in, 48)

                def body(i):
                    for s in range(2):
                        b = i * 2 + s
                        wait_alone(pool, b_in[s], (i + 1) * 48)
                        wait_alone(pool, a_out, (b - 1) * 2)
                        pool.tensor_tensor(xb[:, s], xi[:, s], bob[:, :].unsqueeze(1).to_broadcast([P, TT, D]), ALU.add).then_inc(biased, 1)
                        wait_alone(pool, summed, (b + 1) * 2)
                        pool.dma_start(out[bass.ds(b, 1)].rearrange("o (t p) d -> p (o t) d", p=P), res[:, s]).then_inc(stored[s], 16)

                first_apart(pool, B // 2, body)
                for s in range(2):
                    wait_alone(pool, stored[s], B // 2 * 16)

            @block.vector
            def _(dve):
                dve.wait_ge(const_in, 48)

                def body(i):
                    for s in range(2):
                        b = i * 2 + s
                        dve.wait_ge(rows_in[s], (i + 1) * 32)
                        wait(dve, f_full, b * 2)
                        for e in range(NE):
                            dve.scalar_tensor_tensor(back[:, 0, e], srow[:, s, e], slot_col[:, 0:1], prow[:, s, e],
                                                     ALU.is_equal, ALU.mult).then_inc(placed, 1)
                        dve.wait_ge(biased, b + 1)
                        wait(dve, stored[s], i * 16)
                        for k in range(2):
                            dve.wait_ge(a_full, b * 2 + k + 1)
                            dve.tensor_tensor(res[:, s, 2 * k:2 * k + 2], ap[:, k], xb[:, s, 2 * k:2 * k + 2], ALU.add).then_inc(a_out, 1)
                        dve.wait_ge(a_out, b * 2 + 2)
                        for k in range(2):
                            dve.wait_ge(f_out, b * 2 + k + 1)
                            dve.tensor_tensor(res[:, s, 2 * k:2 * k + 2], res[:, s, 2 * k:2 * k + 2],
                                              ffn[:, s, 2 * k:2 * k + 2], ALU.add).then_inc(summed, 1)

                first_apart(dve, B // 2, body)

            @block.scalar
            def _(act):
                def body(i):
                    for s in range(2):
                        b = i * 2 + s
                        wait(act, summed, (b - 1) * 2)
                        for k in range(2):
                            act.wait_ge(f_full, b * 2 + k + 1)
                            act.activation(ffn[:, s, 2 * k:2 * k + 2], fp[:, 2 * s + k], ACT.Copy).then_inc(f_out, 1)

                first_apart(act, B // 2, body)

            @block.tensor
            def _(pe):
                pe.wait_ge(const_in, 48)

                def body(i):
                    for s in range(2):
                        b = i * 2 + s
                        pe.wait_ge(b_in[s], (i + 1) * 48)
                        wait(pe, a_out, b * 2)
                        for k in range(2):
                            for t in range(2):
                                tok = (2 * k + t) * P
                                for c in range(DC):
                                    ins = pe.matmul(ap[:, k, t], att[:, s, c, tok:tok + P], wo[:, c], start=(c == 0), stop=(c == DC - 1))
                            ins.then_inc(a_full, 1)
                        wait(pe, f_out, (b - 1) * 2)
                        pe.wait_ge(placed, (b + 1) * NE)
                        for k in range(2):
                            for t in range(2):
                                tok = (2 * k + t) * P
                                for e in range(NE):
                                    ins = pe.matmul(fp[:, 2 * s + k, t], back[:, 0, e, tok:tok + P], y[:, s, e], start=(e == 0), stop=(e == NE - 1))
                            ins.then_inc(f_full, 1)

                first_apart(pe, B // 2, body)


def build(nc, x, Wq, bq, Wk, bk, Wv, bv, Wp, bp, Wo, bo, u, v, gate_w, w1, w2, out):
    names = ("sinusoid", "ident", "spread", "slots", "slot_col", "keep")
    c = {n: nc.inline_tensor(a, name=f"const_{n}").ap() for n, a in zip(names, shape_constants())}
    xn_d = nc.dram_tensor("xn_d", [B, P, TT, D], F32).ap()
    xt_d = nc.dram_tensor("xt_d", [B, P, 2, DC, S], F32).ap()
    slot_d = nc.dram_tensor("slot_d", [B * NE, S], F32).ap()
    prob_d = nc.dram_tensor("prob_d", [B * NE, S], F32).ap()
    xin_d = nc.dram_tensor("xin_d", [NE, B, P, DC, CAP], F32).ap()
    y_d = nc.dram_tensor("y_d", [B, CAP, NE, D], F32).ap()
    xs_d = nc.dram_tensor("xs_d", [4, S * (S + 1)], F32).ap()
    att_d = nc.dram_tensor("att_d", [B, D, S], F32).ap()
    with nc.sbuf_tensor("slot_t", [P, B, TT, NE], F32) as slot_t:
        with nc.sbuf_tensor("gate_scores", [P, B, TT, NE], F32) as gate:
            norm_phase(nc, x, gate_w, c["ident"], xn_d, xt_d, gate)
            route_phase(nc, c["ident"], gate, slot_t, slot_d, prob_d)
        gather_phase(nc, c["slots"], slot_t, xn_d, xin_d)
    weights = {"Wq": Wq, "Wk": Wk, "Wv": Wv, "Wp": Wp, "bq": bq, "bk": bk, "bv": bv, "bp": bp,
               "u": u.rearrange("a h b p -> (a h b p)"), "v": v.rearrange("a h b p -> (a h b p)")}
    attention_phase(nc, weights, (c["sinusoid"], c["ident"], c["spread"], c["keep"]), xt_d, xs_d, att_d)
    ffn_phase(nc, w1, w2, xin_d, y_d)
    combine_phase(nc, x, Wo, bo, c["slot_col"], slot_d, prob_d, y_d, att_d, out)


_INS = ["L0_attn_x", "L0_attn_Wq", "L0_attn_bq", "L0_attn_Wk", "L0_attn_bk", "L0_attn_Wv", "L0_attn_bv", "L0_attn_Wp",
        "L0_attn_bp", "L0_attn_Wo", "L0_attn_bo", "L0_attn_u", "L0_attn_v", "L0_ffn_gate_w", "L0_ffn_w1", "L0_ffn_w2"]
_OUTS = [((B, S, D), "float32")]


def kernel(**inputs):
    import numpy as _np
    import concourse.bacc as _bacc
    from concourse import mybir as _mybir
    from concourse.bass_utils import run_bass_kernel_spmd as _run

    nc = _bacc.Bacc("TRN2", target_bir_lowering=False, num_devices=1)
    arrays, args = {}, []
    for name in _INS:
        a = _np.ascontiguousarray(inputs[name])
        arrays[f"in_{name}_dram"] = a
        args.append(nc.dram_tensor(f"in_{name}_dram", a.shape, _mybir.dt.from_np(a.dtype), kind="ExternalInput").ap())
    for i, (shape, dtype) in enumerate(_OUTS):
        dt = _mybir.dt.from_np(_np.dtype(dtype))
        args.append(nc.dram_tensor(f"out_{i}_dram", shape, dt, kind="ExternalOutput").ap())
    build(nc, *args)
    r = _run(nc, [arrays], core_ids=[0])
    got = tuple(r.results[0][f"out_{i}_dram"] for i in range(len(_OUTS)))
    return got[0]
```

```python
from contextlib import ExitStack

import numpy as np

import concourse.bass as bass
from concourse import mybir

ALU = mybir.AluOpType
ACT = mybir.ActivationFunctionType
F32 = mybir.dt.float32
F32R = mybir.dt.float32r
BF16 = mybir.dt.bfloat16
AX_X = mybir.AxisListType.X

P = 128
D = 256
DC = D // P
B = 32
S = 512
TT = S // P
H = 16
HD = D // H
NQ = 4
QH = H // NQ
PH = 2
NP = H // PH
PR = PH * HD
COPIES = P // PR
NE = 8
F = 1024
FC = F // P
CAP = 2 * S // NE
HALF = B // 2
GB = 4
NG = B // GB
EPS = 1e-5
NEG = -3.0e38
SPLITS = ((0, 0), (0, 1), (1, 0))


def wait(eng, sem, value):
    if isinstance(value, int) and value <= 0:
        return
    eng.wait_ge(sem, value)


def wait_alone(eng, sem, value):
    wait(eng, sem, value)
    if not isinstance(value, int):
        eng.nop(nofuse=True)


def first_apart(eng, n, body):
    body(0)
    with eng.Fori(1, n) as i:
        body(i)


def ends_apart(eng, n, body):
    body(0)
    with eng.Fori(1, n - 1) as i:
        body(i)
    body(n - 1)


class Memory:

    def __init__(self, nc, ctx, phase):
        self.nc, self.ctx, self.phase = nc, ctx, phase

    def sb(self, name, shape, dt=F32):
        return self.ctx.enter_context(self.nc.sbuf_tensor(f"{self.phase}_{name}", shape, dt))

    def ps(self, name, shape):
        return self.ctx.enter_context(self.nc.psum_tensor(f"{self.phase}_{name}", shape, F32))

    def sem(self, name):
        return self.ctx.enter_context(self.nc.semaphore(f"{self.phase}_{name}"))


def shape_constants():
    pos = np.arange(S, dtype=np.float32)
    idx = np.arange(D // 2, dtype=np.float32)
    inv = (np.float32(1.0) / np.float32(10000.0) ** (np.float32(2.0) * idx / np.float32(D))).astype(np.float32)
    ang = (pos[:, None] * inv[None, :]).astype(np.float32)
    sinusoid = np.ascontiguousarray(np.concatenate([np.sin(ang), np.cos(ang)], axis=-1).astype(np.float32).T)
    ident = np.eye(P, dtype=np.float32)
    slots = np.tile(np.arange(CAP, dtype=np.float32), (P, 1))
    slot_col = np.arange(P, dtype=np.float32).reshape(P, 1)
    keep = np.zeros((P, PH), np.float32)
    for hh in range(PH):
        for copy in range(COPIES):
            row = copy * PH * HD + HD * hh
            keep[row:row + HD, hh] = 1.0
    return sinusoid, ident, slots, slot_col, keep


def norm_phase(nc, x, gate_w, ident_d, xn_d, xt_d, gate):
    with ExitStack() as ctx:
        m = Memory(nc, ctx, "norm")
        ident = m.sb("ident", [P, P])
        gw = m.sb("gw", [P, DC, NE])
        gws = m.sb("gws", [P, 2, DC, NE], F32R)
        xin = m.sb("xin", [P, 2, TT, D])
        xn = m.sb("xn", [P, 2, TT, D])
        stats = m.sb("stats", [P, 2, TT, 6])
        mv = m.sb("mv", [P, 2, TT, 2])
        sd = m.sb("sd", [P, 2, TT])
        rstd = m.sb("rstd", [P, 2, TT])
        eps = m.sb("eps", [P, 1])
        xts = m.sb("xts", [P, 2, 2, DC, S], F32R)
        tp = m.ps("tp", [P, 2, DC, S])
        gp = m.ps("gp", [P, 2, S])
        const_in = m.sem("const_in")
        split = m.sem("split")
        x_in = [m.sem(f"x_in{s}") for s in range(2)]
        stat = m.sem("stat")
        aggr = m.sem("aggr")
        root = m.sem("root")
        recip = m.sem("recip")
        normed = m.sem("normed")
        turned = m.sem("turned")
        high = m.sem("high")
        low = m.sem("low")
        scored = m.sem("scored")
        kept = m.sem("kept")
        stored = [m.sem(f"stored{s}") for s in range(2)]

        with nc.Block() as block:

            @block.sync
            def _(sp):
                sp.dma_start(ident[:, :], ident_d).then_inc(const_in, 16)
                sp.dma_start(gw[:, :, :], gate_w.rearrange("(c p) e -> p c e", p=P)).then_inc(const_in, 16)

                def body(i):
                    for s in range(2):
                        b = i * 2 + s
                        wait_alone(sp, normed, b + 1)
                        sp.dma_start(xn_d[bass.ds(b, 1)].rearrange("o p t d -> p (o t) d"), xn[:, s]).then_inc(stored[s], 16)
                        wait_alone(sp, low, b + 1)
                        sp.dma_start(xt_d[bass.ds(b, 1)].rearrange("o p k c t -> p (o k) c t"), xts[:, s].bitcast(F32)).then_inc(stored[s], 16)

                first_apart(sp, B // 2, body)
                for s in range(2):
                    sp.wait_ge(stored[s], 32 * (B // 2))

            @block.gpsimd
            def _(pool):
                def body(i):
                    for s in range(2):
                        b = i * 2 + s
                        wait_alone(pool, normed, b - 1)
                        pool.dma_start(xin[:, s], x[bass.ds(b, 1)].rearrange("o (t p) d -> p (o t) d", p=P)).then_inc(x_in[s], 16)

                first_apart(pool, B // 2, body)

            @block.vector
            def _(dve):
                dve.memset(eps[:, :], EPS).then_inc(split, 1)
                dve.wait_ge(const_in, 32)
                dve.tensor_copy(gws[:, 0], gw[:, :, :]).then_inc(split, 1)
                dve.wait_ge(split, 2)
                dve.tensor_tensor(gws[:, 1], gw[:, :, :], gws[:, 0].bitcast(F32), ALU.subtract).then_inc(split, 1)

                def low_part(b, s):
                    dve.wait_ge(high, b + 1)
                    dve.tensor_tensor(xts[:, s, 1], tp[:, s], xts[:, s, 0].bitcast(F32), ALU.subtract).then_inc(low, 1)

                def body(i):
                    for s in range(2):
                        b = i * 2 + s
                        dve.wait_ge(x_in[s], (i + 1) * 16)
                        for t in range(TT):
                            dve.bn_stats(stats[:, s, t], xin[:, s, t]).then_inc(stat, 1)
                        wait_alone(dve, stat, (b + 1) * TT)
                        for t in range(TT):
                            dve.bn_aggr(mv[:, s, t], stats[:, s, t]).then_inc(aggr, 1)
                        if not (isinstance(i, int) and b == 0):
                            low_part(b - 1, 1 - s)
                        dve.wait_ge(root, b + 1)
                        dve.reciprocal(rstd[:, s], sd[:, s]).then_inc(recip, 1)
                        dve.wait_ge(recip, b + 1)
                        wait(dve, stored[s], i * 32)
                        wait(dve, turned, b - 1)
                        for t in range(TT):
                            ins = dve.tensor_scalar(xn[:, s, t], xin[:, s, t], mv[:, s, t, 0:1], rstd[:, s, t:t + 1],
                                                    ALU.subtract, ALU.mult)
                        ins.then_inc(normed, 1)

                first_apart(dve, B // 2, body)
                low_part(B - 1, 1)

            @block.scalar
            def _(act):
                act.wait_ge(split, 1)

                def keep_scores(b, s):
                    act.wait_ge(scored, b + 1)
                    act.activation(gate[:, bass.ds(b, 1)], gp[:, s:s + 1, 0:TT * NE].rearrange("p o (t e) -> p o t e", e=NE),
                                   ACT.Copy).then_inc(kept, 1)

                def body(i):
                    for s in range(2):
                        b = i * 2 + s
                        act.wait_ge(aggr, (b + 1) * TT)
                        act.activation(sd[:, s], mv[:, s, :, 1], ACT.Sqrt, bias=eps[:, :]).then_inc(root, 1)
                        act.wait_ge(turned, b + 1)
                        wait(act, stored[s], i * 32)
                        act.activation(xts[:, s, 0], tp[:, s], ACT.Copy).then_inc(high, 1)
                        if not (isinstance(i, int) and i == 0):
                            keep_scores(b - 2, s)

                first_apart(act, B // 2, body)
                keep_scores(B - 2, 0)
                keep_scores(B - 1, 1)

            @block.tensor
            def _(pe):
                pe.wait_ge(const_in, 32)
                pe.wait_ge(split, 3)

                def scores(b, s):
                    pe.wait_ge(low, b + 1)
                    wait(pe, kept, b - 1)
                    for t in range(TT):
                        for k, (w, a) in enumerate(SPLITS):
                            for c in range(DC):
                                ins = pe.matmul(gp[:, s, t * NE:(t + 1) * NE], xts[:, s, a, c, t * P:(t + 1) * P],
                                                gws[:, w, c, :], start=(k == 0 and c == 0), stop=(k == 2 and c == DC - 1))
                    ins.then_inc(scored, 1)

                def body(i):
                    for s in range(2):
                        b = i * 2 + s
                        pe.wait_ge(normed, b + 1)
                        wait(pe, low, b - 1)
                        for c in range(DC):
                            for t in range(TT):
                                ins = pe.transpose(tp[:, s, c, t * P:(t + 1) * P], xn[:, s, t, c * P:(c + 1) * P], ident[:, :])
                        ins.then_inc(turned, 1)
                        if not (isinstance(i, int) and b == 0):
                            scores(b - 1, 1 - s)

                first_apart(pe, B // 2, body)
                scores(B - 1, 1)


def route_phase(nc, ident_d, gate, slot_t, slot_d, prob_d):
    with ExitStack() as ctx:
        m = Memory(nc, ctx, "route")
        ident = m.sb("ident", [P, P])
        top = m.sb("top", [P, B * TT])
        den = m.sb("den", [P, B * TT])
        inv = m.sb("inv", [P, B * TT])
        probs = m.sb("probs", [P, B, TT, NE])
        by_tile = m.sb("by_tile", [P, TT, B, NE])
        rows = m.sb("rows", [P, 2, S])
        work = m.sb("work", [P, 2, S])
        best = m.sb("best", [P, 2, 8])
        mask = m.sb("mask", [P, 2, S])
        ones = m.sb("ones", [P, S])
        order = m.sb("order", [P, 2, S])
        slot = m.sb("slot", [P, 2, S])
        slot_b = m.sb("slot_b", [P, 2, S], BF16)
        tp = m.ps("tp", [P, 2, S])
        tb = m.ps("tb", [P, 2, S])
        const_in = m.sem("const_in")
        step = m.sem("step")
        exped = m.sem("exped")
        turned = m.sem("turned")
        row = m.sem("row")
        taken = [m.sem(f"taken{h}") for h in range(2)]
        slotted = m.sem("slotted")
        back = m.sem("back")
        stored = m.sem("stored")
        g3 = gate[:, :, :, :].rearrange("p b t e -> p (b t) e")
        p3 = probs[:, :, :, :].rearrange("p b t e -> p (b t) e")

        with nc.Block() as block:

            @block.sync
            def _(sp):
                sp.dma_start(ident[:, :], ident_d).then_inc(const_in, 16)
                wait_alone(sp, row, 2)
                sp.dma_start(prob_d.rearrange("(h r) t -> r h t", h=2), rows[:, :, :]).then_inc(stored, 16)
                wait_alone(sp, slotted, 2)
                sp.dma_start(slot_d.rearrange("(h r) t -> r h t", h=2), slot_b[:, :, :]).then_inc(stored, 16)
                wait_alone(sp, stored, 32)

            @block.vector
            def _(dve):
                dve.memset(ones[:, :], 1.0)
                dve.tensor_reduce(top[:, :], g3, AX_X, ALU.max).then_inc(step, 1)
                dve.wait_ge(step, 1)
                spread = top[:, :].unsqueeze(2).to_broadcast([P, B * TT, NE])
                dve.tensor_tensor(p3, g3, spread, ALU.subtract).then_inc(step, 1)
                dve.wait_ge(exped, 1)
                dve.tensor_reduce(den[:, :], p3, AX_X, ALU.add).then_inc(step, 1)
                dve.wait_ge(step, 3)
                dve.reciprocal(inv[:, :], den[:, :]).then_inc(step, 1)
                dve.wait_ge(step, 4)
                dve.tensor_tensor(by_tile[:, :, :, :].rearrange("p t b e -> p b t e"), probs[:, :, :, :],
                                  inv[:, :].rearrange("p (b t) -> p b t", t=TT).unsqueeze(3).to_broadcast([P, B, TT, NE]),
                                  ALU.mult).then_inc(step, 1)
                dve.wait_ge(turned, 1)
                for h in range(2):
                    dve.tensor_copy(rows[:, h], tp[:, h]).then_inc(row, 1)
                dve.wait_ge(row, 2)
                for k in range(CAP // 8):
                    for h in range(2):
                        src = rows if k == 0 else work
                        if k:
                            dve.wait_ge(taken[h], 2 * k)
                        dve.max(best[:, h], src[:, h]).then_inc(taken[h], 1)
                    for h in range(2):
                        src = rows if k == 0 else work
                        dve.wait_ge(taken[h], 2 * k + 1)
                        dve.match_replace(work[:, h], best[:, h], src[:, h], -1.0).then_inc(taken[h], 1)
                for h in range(2):
                    dve.wait_ge(taken[h], 2 * (CAP // 8))
                    dve.tensor_scalar(mask[:, h], work[:, h], 0.0, None, ALU.is_lt).then_inc(taken[h], 1)
                    dve.wait_ge(taken[h], 2 * (CAP // 8) + 1)
                    dve.tensor_tensor_scan(order[:, h], ones[:, :], mask[:, h], 0.0, ALU.mult, ALU.add).then_inc(taken[h], 1)
                    dve.wait_ge(taken[h], 2 * (CAP // 8) + 2)
                    dve.tensor_tensor(order[:, h], order[:, h], mask[:, h], ALU.mult).then_inc(taken[h], 1)
                    dve.wait_ge(taken[h], 2 * (CAP // 8) + 3)
                    dve.tensor_scalar(slot_b[:, h], order[:, h], -1.0, None, ALU.add)
                    dve.tensor_scalar(slot[:, h], order[:, h], -1.0, None, ALU.add).then_inc(slotted, 1)
                dve.wait_ge(back, 1)
                for h in range(2):
                    dve.tensor_copy(slot_t[:, h * HALF:(h + 1) * HALF].rearrange("p b t e -> p t b e"),
                                    tb[:, h].rearrange("p (t b e) -> p t b e", t=TT, e=NE))

            @block.scalar
            def _(act):
                act.wait_ge(step, 2)
                act.activation(p3, p3, ACT.Exp).then_inc(exped, 1)

            @block.tensor
            def _(pe):
                pe.wait_ge(const_in, 16)
                pe.wait_ge(step, 5)
                for h in range(2):
                    for t in range(TT):
                        ins = pe.transpose(tp[:, h, t * P:(t + 1) * P],
                                           by_tile[:, t, h * HALF:(h + 1) * HALF, :].rearrange("p b e -> p (b e)"), ident[:, :])
                ins.then_inc(turned, 1)
                pe.wait_ge(slotted, 2)
                for h in range(2):
                    for t in range(TT):
                        ins = pe.transpose(tb[:, h, t * P:(t + 1) * P], slot[:, h, t * P:(t + 1) * P], ident[:, :])
                ins.then_inc(back, 1)


def gather_phase(nc, slots_d, slot_t, xn_d, xin_d):
    with ExitStack() as ctx:
        m = Memory(nc, ctx, "gather")
        slots = m.sb("slots", [P, CAP])
        xn = m.sb("xn", [P, 2, TT, D])
        xs = m.sb("xs", [P, 2, 2, TT, D], F32R)
        pick = m.sb("pick", [P, 2, TT, NE, CAP], F32R)
        out = m.sb("out", [P, 2, DC, NE, CAP])
        gp = m.ps("gp", [P, 2, 4, S])
        const_in = m.sem("const_in")
        x_in = [m.sem(f"x_in{s}") for s in range(2)]
        high = m.sem("high")
        low = m.sem("low")
        picked = m.sem("picked")
        gathered = m.sem("gathered")
        out_a = m.sem("out_a")
        out_b = m.sem("out_b")
        stored = [m.sem(f"stored{s}") for s in range(2)]

        def compare(eng, t, s, b):
            return eng.tensor_tensor(pick[:, s, t],
                                     slots[:, :].unsqueeze(1).to_broadcast([P, NE, CAP]),
                                     slot_t[:, bass.ds(b, 1), t, :].rearrange("p o e -> p (o e)").unsqueeze(2).to_broadcast([P, NE, CAP]),
                                     ALU.is_equal)

        with nc.Block() as block:

            @block.sync
            def _(sp):
                sp.dma_start(slots[:, :], slots_d).then_inc(const_in, 16)

                def body(i):
                    for s in range(2):
                        b = i * 2 + s
                        wait_alone(sp, out_a, (b + 1) * 2)
                        wait_alone(sp, out_b, (b + 1) * 2)
                        for c in range(DC):
                            sp.dma_start(xin_d[:, bass.ds(b, 1), :, c].rearrange("e o p k -> p (o e) k"), out[:, s, c]).then_inc(stored[s], 16)

                first_apart(sp, B // 2, body)
                for s in range(2):
                    sp.wait_ge(stored[s], 32 * (B // 2))

            @block.gpsimd
            def _(pool):
                def body(i):
                    for s in range(2):
                        b = i * 2 + s
                        wait_alone(pool, low, b - 1)
                        pool.dma_start(xn[:, s], xn_d[bass.ds(b, 1)].rearrange("o p t d -> p (o t) d")).then_inc(x_in[s], 16)

                first_apart(pool, B // 2, body)

            @block.vector
            def _(dve):
                dve.wait_ge(const_in, 16)

                def evacuate(b, s, turn):
                    wait(dve, stored[s], turn * 32)
                    for k in (0, 2):
                        dve.wait_ge(gathered, b * 4 + k + 1)
                        dve.tensor_copy(out[:, s, k // 2, 0:4], gp[:, s, k].rearrange("p (e k) -> p e k", e=4)).then_inc(out_a, 1)

                def body(i):
                    for s in range(2):
                        b = i * 2 + s
                        wait(dve, gathered, (b - 1) * 4)
                        for t in range(TT):
                            compare(dve, t, s, b).then_inc(picked, 1)
                        dve.wait_ge(high, b + 1)
                        dve.tensor_tensor(xs[:, s, 1], xn[:, s], xs[:, s, 0].bitcast(F32), ALU.subtract).then_inc(low, 1)
                        if not (isinstance(i, int) and b == 0):
                            evacuate(b - 1, 1 - s, i + s - 1)

                first_apart(dve, B // 2, body)
                evacuate(B - 1, 1, B // 2 - 1)

            @block.scalar
            def _(act):
                def evacuate(b, s, turn):
                    wait(act, stored[s], turn * 32)
                    for k in (1, 3):
                        act.wait_ge(gathered, b * 4 + k + 1)
                        act.activation(out[:, s, k // 2, 4:8], gp[:, s, k].rearrange("p (e k) -> p e k", e=4),
                                       ACT.Copy).then_inc(out_b, 1)

                def body(i):
                    for s in range(2):
                        b = i * 2 + s
                        act.wait_ge(x_in[s], (i + 1) * 16)
                        wait(act, gathered, (b - 1) * 4)
                        act.activation(xs[:, s, 0], xn[:, s], ACT.Copy).then_inc(high, 1)
                        if not (isinstance(i, int) and b == 0):
                            evacuate(b - 1, 1 - s, i + s - 1)

                first_apart(act, B // 2, body)
                evacuate(B - 1, 1, B // 2 - 1)

            @block.tensor
            def _(pe):
                def body(i):
                    for s in range(2):
                        b = i * 2 + s
                        pe.wait_ge(picked, (b + 1) * TT)
                        pe.wait_ge(low, b + 1)
                        wait(pe, out_a, (b - 1) * 2)
                        wait(pe, out_b, (b - 1) * 2)
                        for k in range(4):
                            c, q = k // 2, k % 2
                            for t in range(TT):
                                for a in range(2):
                                    ins = pe.matmul(gp[:, s, k], xs[:, s, a, t, c * P:(c + 1) * P],
                                                    pick[:, s, t, q * 4:(q + 1) * 4, :],
                                                    start=(t == 0 and a == 0), stop=(t == TT - 1 and a == 1))
                            ins.then_inc(gathered, 1)

                first_apart(pe, B // 2, body)


def attention_phase(nc, w, consts, xt_d, xs_d, att_d, sums_d):
    sin_d, ident_d, keep_d = consts
    LEAD = 3
    LAG = 2
    NX = 4
    UNITS = B * NQ
    with ExitStack() as ctx:
        m = Memory(nc, ctx, "att")
        ident = m.sb("ident", [P, P])
        keep = m.sb("keep", [P, PH])
        bias_u = m.sb("bias_u", [P, NP])
        bias_v = m.sb("bias_v", [P, NP])
        bias_k = m.sb("bias_k", [P, NP])
        bias_p = m.sb("bias_p", [P, NP])
        raw = m.sb("raw", [P, 3, NP])
        bv = m.sb("bv", [P, D])
        wq = m.sb("wq", [P, 2, DC, NP, P], F32R)
        wk = m.sb("wk", [P, 2, DC, NP, P], F32R)
        wv = m.sb("wv", [P, 2, DC, D], F32R)
        pos = m.sb("pos", [P, NP, S], F32R)
        shared = m.sb("shared", [P, 4, TT, S])
        shifted = m.sb("shifted", [P, NX, TT, S])
        wst = shared[:, :, 0, :].rearrange("p k (c n) -> p k c n", c=DC)
        sinus = shifted[:, 0].rearrange("p t s -> p (t s)")[:, 0:DC * S].rearrange("p (c s) -> p c s", c=DC)
        wpd = shifted[:, 1].rearrange("p t s -> p (t s)")[:, 0:DC * NP * P].rearrange("p (c q n) -> p c q n", c=DC, q=NP)

        xt = m.sb("xt", [P, 2, DC, S], F32R)
        qd = m.sb("qd", [P, 2, 2, S], F32R)
        kd = m.sb("kd", [P, 4, S], F32R)
        qu = m.sb("qu", [P, QH, S], F32R)
        qv = m.sb("qv", [P, QH, S], F32R)
        vst = m.sb("vst", [P, TT, D])
        val = m.sb("val", [P, TT, H, 32])
        xo = m.sb("xo", [P, 2, TT, S + 1])
        mx = m.sb("mx", [P, 4, TT])
        nm = m.sb("nm", [P, 4, TT])
        pt = m.sb("pt", [P, 2, TT, S])
        osb = m.sb("osb", [P, 2, QH, P])

        xp = m.ps("xp", [P, 2, S])
        sp_ = m.ps("sp", [P, 2, S])
        tp = m.ps("tp", [P, 2, S])
        op = m.ps("op", [P, S])
        mp = m.ps("mp", [P, S])

        const_in = m.sem("const_in")
        set_up = m.sem("set_up")
        set_hi = m.sem("set_hi")
        p_full = m.sem("p_full")
        p_hi = m.sem("p_hi")
        p_lo = m.sem("p_lo")
        ones_set = m.sem("ones_set")
        edge_set = m.sem("edge_set")
        xt_in = m.sem("xt_in")
        q_full = m.sem("q_full")
        q_high = m.sem("q_high")
        q_low = m.sem("q_low")
        k_full = m.sem("k_full")
        k_high = m.sem("k_high")
        k_low = m.sem("k_low")
        v_full = m.sem("v_full")
        v_staged = m.sem("v_staged")
        v_ready = m.sem("v_ready")
        qv_ready = m.sem("qv_ready")
        qu_ready = m.sem("qu_ready")
        x_full = m.sem("x_full")
        x_out = m.sem("x_out")
        x_written = [m.sem(f"x_written{k}") for k in range(NX)]
        x_shifted = [m.sem(f"x_shifted{k}") for k in range(NX)]
        s_full = m.sem("s_full")
        added = m.sem("added")
        max_ready = m.sem("max_ready")
        exp_done = m.sem("exp_done")
        t_full = m.sem("t_full")
        t_out_dve = m.sem("t_out_dve")
        t_out_act = m.sem("t_out_act")
        o_full = m.sem("o_full")
        o_out = m.sem("o_out")
        o_stored = [m.sem(f"o_stored{k}") for k in range(2)]

        def queries_at(k, last):
            return k // 2 + 2 if k % 2 == 0 and not (last and k + 4 >= H) else None

        def keys_at(k, last):
            if k in (H - 8, H - 7):
                return NP - 2 + k - (H - 8)
            return k // 2 + 2 if k % 2 and k != H - 5 and not (last and k + 3 >= H) else None

        def values_at(k, last):
            return {H - 3: 0, H - 1: 1}.get(k) if not last else None

        def columns(vector):
            return vector.rearrange("(q n) -> n q", q=NP)

        def copies(weight):
            return weight.rearrange("p (q n) -> p q n", q=NP).unsqueeze(2).to_broadcast([P, NP, COPIES, PR])

        def of_copies(tile):
            return tile.rearrange("p q (r n) -> p q r n", r=COPIES)

        with nc.Block() as block:

            @block.sync
            def _(sp):
                sp.dma_start(ident[:, :], ident_d).then_inc(const_in, 16)
                sp.dma_start(keep[:, :], keep_d).then_inc(const_in, 16)
                sp.dma_start(sinus, sin_d.rearrange("(c p) t -> p c t", p=P)).then_inc(const_in, 16)
                for k, name in enumerate(("Wq", "Wk", "Wv", "Wp")):
                    sp.dma_start(wst[:, k], w[name].rearrange("(c p) n -> p c n", p=P)).then_inc(const_in, 16)
                for copy in range(COPIES):
                    rows = slice(PR * copy, PR * (copy + 1))
                    for to, name in ((raw[rows, 0], "bq"), (raw[rows, 1], "u"), (raw[rows, 2], "v"),
                                     (bias_k[rows], "bk"), (bias_p[rows], "bp")):
                        sp.dma_start(to, columns(w[name]), allow_slow_non_contiguous=True).then_inc(const_in, 16)
                sp.dma_start(bv[:, :], w["bv"].partition_broadcast(P)).then_inc(const_in, 16)

                def load_xt(b):
                    sp.dma_start(xt[:, :, :, :].bitcast(F32), xt_d[bass.ds(b, 1)].rearrange("o p k c t -> p (o k) c t")).then_inc(xt_in, 16)

                def write_x(b, k, half):
                    slot, turn = k % NX, b * NQ + k // NX
                    tiles = slice(2 * half, 2 * half + 2)
                    wait_alone(sp, x_out, (b * H + k) * 2 + half + 1)
                    if half == 0:
                        wait_alone(sp, x_shifted[slot], turn * 16)
                    sp.dma_start(xs_d[slot].rearrange("(t p c) -> p t c", t=TT, c=S + 1)[:, tiles], xo[:, k % 2, tiles]
                                 ).then_inc(x_written[slot], 16)

                def read_x(b, k):
                    slot, turn = k % NX, b * NQ + k // NX
                    wait_alone(sp, x_written[slot], (turn + 1) * 32)
                    wait_alone(sp, added, (b * H + k - NX + 1) * TT)
                    sp.dma_start(shifted[:, slot], xs_d[slot][S:S + S * S].rearrange("(t p c) -> p t c", t=TT, c=S)).then_inc(x_shifted[slot], 16)

                def store_o(b, q):
                    wait_alone(sp, o_out, b * NQ + q + 1)
                    at = bass.ds(b + q // NQ, 1)
                    dst = att_d[at].rearrange("o (q h v) t -> (o q) v h t", q=NQ, h=QH)
                    for t in range(TT):
                        sp.dma_start(dst[q % NQ, :, :, t * P:(t + 1) * P], osb[32 * t:32 * t + HD, q % 2]).then_inc(o_stored[q % 2], 16)
                    for t in range(TT):
                        row = 32 * t + HD
                        sp.dma_start(sums_d[at].rearrange("o (q h) t -> (o q) h t", q=NQ)[q % NQ:q % NQ + 1, :, t * P:(t + 1) * P],
                                     osb[row:row + 1, q % 2]).then_inc(o_stored[q % 2], 16)

                load_xt(0)
                sp.wait_ge(p_lo, 2 * NP)
                sp.wait_ge(set_up, SET_UP)
                for k in range(LEAD):
                    write_x(0, k, 0)
                    if k:
                        read_x(0, k - 1)
                    write_x(0, k, 1)

                def body(b):
                    first = isinstance(b, int) and b == 0
                    last = isinstance(b, int) and b == B - 1
                    for k in range(H):
                        if k == H - 6 and not last:
                            wait_alone(sp, q_full, b * NP + NP)
                            load_xt(b + 1)
                        if not (last and k + LEAD >= H):
                            write_x(b, k + LEAD, 0)
                        if not (last and k + LEAD - 1 >= H):
                            read_x(b, k + LEAD - 1)
                        if not (last and k + LEAD >= H):
                            write_x(b, k + LEAD, 1)
                        if k % QH == 0 and not (first and k < 2 * QH):
                            store_o(b, k // QH - 2)

                ends_apart(sp, B, body)
                store_o(B - 1, NQ - 2)
                store_o(B - 1, NQ - 1)
                for k in range(2):
                    sp.wait_ge(o_stored[k], UNITS // 2 * 2 * TT * 16)

            @block.gpsimd
            def _(pool):
                pool.memset(val[:, :, :, :], 0.0).then_inc(ones_set, 1)
                wait_alone(pool, ones_set, 1)
                pool.memset(val[:, :, :, HD:HD + 1], 1.0).then_inc(ones_set, 1)
                pool.memset(xo[:, :, :, 0:1], 0.0).then_inc(edge_set, 1)
                wait_alone(pool, const_in, 16 * CONST_LOADS)

                def keep_head(dst, src, h, slot):
                    return pool.tensor_scalar(dst[:, slot], src.bitcast(F32), keep[:, h:h + 1], None, ALU.mult)

                def heads_v(b, p):
                    v = b * NP + p
                    wait_alone(pool, q_low, v * 2 + 2)
                    for h in range(PH):
                        wait_alone(pool, x_full, (v * PH + h - 3) * 2)
                        keep_head(qv, qd[:, p % 2, 1], h, (p * PH + h) % 4).then_inc(qv_ready, 1)

                def head_u(b, p, h):
                    v = b * NP + p
                    wait_alone(pool, s_full, (v * PH + h - 3) * TT)
                    keep_head(qu, qd[:, p % 2, 0], h, (p * PH + h) % 4).then_inc(qu_ready, 1)

                for p in range(2):
                    heads_v(0, p)
                    head_u(0, p, 0)
                    head_u(0, p, 1)

                def body(b):
                    last = isinstance(b, int) and b == B - 1
                    for p in range(NP):
                        ahead = not (last and p + 2 >= NP)
                        if ahead:
                            heads_v(b, p + 2)
                            head_u(b, p + 2, 0)
                            head_u(b, p + 2, 1)

                ends_apart(pool, B, body)

            @block.scalar
            def _(act):
                act.wait_ge(const_in, 16 * CONST_LOADS)
                for c in range(DC):
                    act.activation(of_copies(wq[:, 0, c]), copies(wst[:, 0, c]), ACT.Copy).then_inc(set_hi, 1)
                    act.activation(of_copies(wk[:, 0, c]), copies(wst[:, 1, c]), ACT.Copy).then_inc(set_hi, 1)
                    act.activation(of_copies(wpd[:, c]), copies(wst[:, 3, c]), ACT.Copy).then_inc(set_hi, 1)
                act.activation(wv[:, 0], wst[:, 2], ACT.Copy).then_inc(set_hi, 1)
                for p in range(NP):
                    act.wait_ge(p_full, p + 1)
                    act.activation(pos[:, p], (mp, op)[p % 2][:, :], ACT.Identity, bias=bias_p[:, p:p + 1]).then_inc(p_hi, 1)

                def q_highs(b, p):
                    v = b * NP + p
                    act.wait_ge(q_full, v + 1)
                    wait(act, qu_ready, (v - 1) * PH)
                    for k, bias in enumerate((bias_u, bias_v)):
                        act.activation(qd[:, p % 2, k], mp[:, :], ACT.Identity, bias=bias[:, p % NP:p % NP + 1]).then_inc(q_high, 1)

                def k_highs(b, p):
                    v = b * NP + p
                    act.wait_ge(k_full, v + 1)
                    wait(act, s_full, (v - 3) * PH * TT)
                    act.activation(kd[:, p % 4], mp[:, :], ACT.Identity, bias=bias_k[:, p % NP:p % NP + 1]).then_inc(k_high, 1)

                def x_evacuate(b, k, half):
                    n = b * H + k
                    if half == 0 and not (isinstance(b, int) and b * H + k < 2):
                        act.wait_ge(x_written[(k - 2) % NX], (b * NQ + (k - 2) // NX + 1) * 32)
                    act.wait_ge(x_full, n * 2 + half + 1)
                    act.activation(xo[:, k % 2, 2 * half:2 * half + 2, 1:S + 1], xp[:, :, :], ACT.Copy).then_inc(x_out, 1)

                def exponentials(b, k, half):
                    act.wait_ge(max_ready, b * H + k + 1)
                    for t in (2 * half, 2 * half + 1):
                        act.activation(shared[:, k % 4, t], shared[:, k % 4, t], ACT.Exp, bias=nm[:, k % 4, t:t + 1],
                                       scale=0.25).then_inc(exp_done, 1)

                def t_evacuate(b, k):
                    n = b * H + k
                    act.wait_ge(t_full, (n + 1) * TT)
                    wait(act, o_full, n - 1)
                    act.activation(pt[:, k % 2, TT - 1], tp[:, 1], ACT.Copy).then_inc(t_out_act, 1)

                def values(b):
                    act.wait_ge(v_staged, b * 2 + 2)
                    wait(act, o_full, b * H)
                    for c in range(2):
                        ins = act.activation(val[:, 2 * c:2 * c + 2, :, 0:HD],
                                             vst[:, 2 * c:2 * c + 2].rearrange("p t (h v) -> p t h v", h=H), ACT.Copy)
                    ins.then_inc(v_ready, 1)

                def o_evacuate(b, q):
                    u = b * NQ + q
                    act.wait_ge(o_full, (u + 1) * QH)
                    wait(act, o_stored[q % 2], (u - q % 2) * (TT * 16))
                    act.activation(osb[:, q % 2].rearrange("p h t -> p (h t)"), op[:, :], ACT.Copy).then_inc(o_out, 1)

                act.wait_ge(set_up, 2)
                act.wait_ge(edge_set, 1)
                act.wait_ge(ones_set, 2)
                for p in range(2):
                    q_highs(0, p)
                    k_highs(0, p)
                for k in range(LEAD):
                    x_evacuate(0, k, 0)
                    x_evacuate(0, k, 1)

                def body(b):
                    first = isinstance(b, int) and b == 0
                    last = isinstance(b, int) and b == B - 1
                    for k in range(H):
                        q, hh = k // QH, k % QH
                        queries, keys = queries_at(k, last), keys_at(k, last)
                        positions = not (last and k + LEAD >= H)
                        if k == LAG:
                            values(b)
                        if not (first and k == 0):
                            exponentials(b, k - 1, 0)
                        if queries:
                            q_highs(b, queries)
                        if positions:
                            x_evacuate(b, k + LEAD, 0)
                        if hh == 2 and not (first and q == 0):
                            o_evacuate(b, q - 1)
                        if not (first and k == 0):
                            exponentials(b, k - 1, 1)
                        if keys:
                            k_highs(b, keys)
                        if not (first and k < LAG):
                            t_evacuate(b, k - LAG)
                        if positions:
                            x_evacuate(b, k + LEAD, 1)

                ends_apart(act, B, body)
                exponentials(B, -1, 0)
                exponentials(B, -1, 1)
                for k in range(LAG):
                    t_evacuate(B, k - LAG)
                o_evacuate(B - 1, NQ - 1)

            @block.vector
            def _(dve):
                dve.wait_ge(const_in, 16 * CONST_LOADS)
                dve.tensor_tensor(bias_u[:, :], raw[:, 0], raw[:, 1], ALU.add).then_inc(set_up, 1)
                dve.tensor_tensor(bias_v[:, :], raw[:, 0], raw[:, 2], ALU.add).then_inc(set_up, 1)
                dve.wait_ge(set_up, 2)
                dve.wait_ge(set_hi, 3 * DC + 1)
                for c in range(DC):
                    for k, weight in enumerate((wq, wk)):
                        dve.tensor_tensor(of_copies(weight[:, 1, c]), copies(wst[:, k, c]), of_copies(weight[:, 0, c]).bitcast(F32),
                                          ALU.subtract).then_inc(set_up, 1)
                dve.tensor_tensor(wv[:, 1], wst[:, 2], wv[:, 0].bitcast(F32), ALU.subtract).then_inc(set_up, 1)
                dve.wait_ge(set_up, SET_UP)

                def to_low(part, bias, rows, bank=mp):
                    return dve.scalar_tensor_tensor(part[rows], bank[rows], bias[rows], part[rows].bitcast(F32), ALU.add, ALU.subtract)

                KEY_LOWS = (slice(PR, 2 * PR), slice(3 * PR, P))
                QUERY_LOWS = slice(2 * PR, P)

                for p in range(NP):
                    dve.wait_ge(p_hi, p + 1)
                    for rows in KEY_LOWS:
                        to_low(pos[:, p], bias_p[:, p:p + 1], rows, (mp, op)[p % 2]).then_inc(p_lo, 1)

                def q_lows(b, p):
                    v = b * NP + p
                    dve.wait_ge(q_high, v * 2 + 2)
                    for k, bias in enumerate((bias_u, bias_v)):
                        to_low(qd[:, p % 2, k], bias[:, p % NP:p % NP + 1], QUERY_LOWS).then_inc(q_low, 1)

                def k_lows(b, p):
                    dve.wait_ge(k_high, b * NP + p + 1)
                    for rows in KEY_LOWS:
                        to_low(kd[:, p % 4], bias_k[:, p % NP:p % NP + 1], rows).then_inc(k_low, 1)

                def stage_v(b, half):
                    dve.wait_ge(v_full, b * 2 + half + 1)
                    wait(dve, v_ready, b)
                    dve.tensor_tensor(vst[:, 2 * half:2 * half + 2], mp[:, :].rearrange("p (t n) -> p t n", t=2),
                                      bv[:, :].unsqueeze(1).to_broadcast([P, 2, D]), ALU.add).then_inc(v_staged, 1)

                def add(b, k, t):
                    n = b * H + k
                    if t == 0:
                        dve.wait_ge(x_shifted[k % NX], (b * NQ + k // NX + 1) * 16)
                        wait(dve, t_full, (n - 3) * TT)
                    wait_alone(dve, s_full, n * TT + t + 1)
                    dve.tensor_tensor_reduce(out=shared[:, k % 4, t], in0=sp_[:, t % 2], in1=shifted[:, k % NX, t], scale=1.0,
                                             scalar=NEG, op0=ALU.add, op1=ALU.max,
                                             accum_out=mx[:, k % 4, t:t + 1]).then_inc(added, 1)

                def t_evacuate(b, k, t):
                    n = b * H + k
                    dve.wait_ge(t_full, n * TT + t + 1)
                    if t == 0:
                        wait(dve, o_full, n - 1)
                    dve.tensor_copy(pt[:, k % 2, t], tp[:, t % 2]).then_inc(t_out_dve, 1)

                for p in range(2):
                    q_lows(0, p)
                    k_lows(0, p)
                stage_v(0, 0)
                stage_v(0, 1)

                def body(b):
                    first = isinstance(b, int) and b == 0
                    last = isinstance(b, int) and b == B - 1
                    for k in range(H):
                        n = b * H + k
                        queries, keys = queries_at(k, last), keys_at(k, last)
                        half = values_at(k, last)
                        for t in range(TT):
                            add(b, k, t)
                            if t == 1 and half is not None:
                                stage_v(b + 1, half)
                            if t == TT - 1:
                                dve.wait_ge(added, n * TT + TT)
                                dve.tensor_scalar(nm[:, k % 4], mx[:, k % 4], -0.25, None, ALU.mult).then_inc(max_ready, 1)
                            if t < TT - 1 and not (first and k < LAG):
                                t_evacuate(b, k - LAG, t)
                            if t == 1 and queries:
                                q_lows(b, queries)
                            if t == TT - 1 and keys:
                                k_lows(b, keys)

                ends_apart(dve, B, body)
                for k in range(LAG):
                    for t in range(TT - 1):
                        t_evacuate(B, k - LAG, t)

            @block.tensor
            def _(pe):
                pe.wait_ge(const_in, 16 * CONST_LOADS)
                pe.wait_ge(set_hi, 3 * DC + 1)
                for q in range(NP):
                    wait(pe, p_lo, 2 * (q - 1))
                    for c in range(DC):
                        ins = pe.matmul((mp, op)[q % 2][:, :], wpd[:, c, q, :], sinus[:, c, :], start=(c == 0), stop=(c == DC - 1))
                    ins.then_inc(p_full, 1)
                pe.wait_ge(set_up, SET_UP)
                pe.wait_ge(p_lo, 2 * NP)

                def project(weight, p, sem):
                    for k, (wi, xi) in enumerate(SPLITS):
                        for c in range(DC):
                            ins = pe.matmul(mp[:, :], weight[:, wi, c, p % NP, :], xt[:, xi, c, :],
                                            start=(k == 0 and c == 0), stop=(k == 2 and c == DC - 1))
                    ins.then_inc(sem, 1)


                def project_q(b, p, after_v):
                    pe.wait_ge(xt_in, (b + 1 + p // NP) * 16)
                    wait(pe, k_low, (b * NP + p + (p == NP - 1)) * 2)
                    wait(pe, v_staged, after_v)
                    project(wq, p, q_full)

                def project_k(b, p, after_v):
                    pe.wait_ge(q_low, (b * NP + p + (p != NP - 1)) * 2)
                    wait(pe, k_low, (b * NP + p) * 2)
                    wait(pe, v_staged, after_v)
                    project(wk, p, k_full)

                def project_v(b, half, after, low):
                    pe.wait_ge(low, after)
                    wait(pe, v_staged, b * 2 + half)
                    for t in range(2):
                        tok = (2 * half + t) * P
                        for k, (wi, xi) in enumerate(SPLITS):
                            for c in range(DC):
                                ins = pe.matmul(mp[:, t * D:(t + 1) * D], xt[:, xi, c, tok:tok + P], wv[:, wi, c, :],
                                                start=(k == 0 and c == 0), stop=(k == 2 and c == DC - 1))
                    ins.then_inc(v_full, 1)

                def position(b, k, half):
                    n = b * H + k
                    if half == 0:
                        pe.wait_ge(qv_ready, n + 1)
                    wait(pe, x_out, n * 2 + half)
                    for t in range(2):
                        tok = (2 * half + t) * P
                        ins = pe.matmul(xp[:, t, :], qv[:, k % 4, tok:tok + P], pos[:, k // PH % NP, :], start=True, stop=True)
                    ins.then_inc(x_full, 1)

                def content(b, k, t):
                    n = b * H + k
                    if t == 0:
                        pe.wait_ge(qu_ready, n + 1)
                        pe.wait_ge(k_low, (b * NP + k // PH + 1) * 2)
                    wait(pe, added, n * TT + t - 1)
                    pe.matmul(sp_[:, t % 2, :], qu[:, k % 4, t * P:(t + 1) * P], kd[:, k // PH % 4, :],
                              start=True, stop=True).then_inc(s_full, 1)

                def turn(b, k, c):
                    n = b * H + k
                    pe.wait_ge(exp_done, (n + 1) * TT)
                    if c == 1:
                        wait(pe, t_out_act, n)
                    else:
                        wait(pe, t_out_dve, n * (TT - 1) + max(c - 1, 0))
                    for t in range(TT):
                        ins = pe.transpose(tp[:, c % 2, t * P:(t + 1) * P], shared[:, k % 4, t, c * P:(c + 1) * P], ident[:, :])
                    ins.then_inc(t_full, 1)

                def times_values(b, k):
                    n = b * H + k
                    pe.wait_ge(v_ready, b + (1 if k >= 0 else 0))
                    if k % QH == 0:
                        wait(pe, o_out, b * NQ + k // QH)
                    for c in range(TT):
                        if c < TT - 1:
                            pe.wait_ge(t_out_dve, n * (TT - 1) + c + 1)
                        else:
                            pe.wait_ge(t_out_act, n + 1)
                        for t in range(TT):
                            ins = pe.matmul(op[32 * t:32 * t + 32, k % QH * P:(k % QH + 1) * P], val[:, c, k % H, :],
                                            pt[:, k % 2, c, t * P:(t + 1) * P], start=(c == 0), stop=(c == TT - 1))
                    ins.then_inc(o_full, 1)

                for p in range(2):
                    project_q(0, p, 0)
                    project_k(0, p, 0)
                project_v(0, 0, 4, k_low)
                project_v(0, 1, 4, k_low)
                for k in range(LEAD):
                    position(0, k, 0)
                    position(0, k, 1)

                def body(b):
                    first = isinstance(b, int) and b == 0
                    last = isinstance(b, int) and b == B - 1
                    for k in range(H):
                        queries, keys = queries_at(k, last), keys_at(k, last)
                        half = values_at(k, last)
                        for t in range(TT):
                            if t:
                                content(b, k, t)
                            if not (first and k < LAG):
                                turn(b, k - LAG, t)
                            if t == 0 and queries:
                                project_q(b, queries, b * 2 + 2 + (k == H - 2))
                            if t == 0 and half is not None:
                                project_v(b + 1, half, (b * NP + NP + half + 1) * 2, q_low)
                            if t % 2 and not (last and k + LEAD >= H):
                                position(b, k + LEAD, t // 2)
                            if t == 2 and keys:
                                project_k(b, keys, 0 if half is None else b * 2 + 3 + half)
                        if not (last and k == H - 1):
                            content(b, k + 1, 0)
                        if not (first and k < LAG):
                            times_values(b, k - LAG)

                content(0, 0, 0)
                ends_apart(pe, B, body)
                for k in range(LAG):
                    for t in range(TT):
                        turn(B, k - LAG, t)
                    times_values(B, k - LAG)


CONST_LOADS = 3 + 4 + COPIES * 5 + 1
SET_UP = 2 + 2 * DC + 1


def ffn_phase(nc, w1, w2, xin_d, routes, y_d, sums_d, inv_d):
    with ExitStack() as ctx:
        m = Memory(nc, ctx, "ffn")
        w1s = m.sb("w1s", [P, DC, F])
        w2s = m.sb("w2s", [P, FC, D])
        w1p = m.sb("w1p", [P, 2, DC, F], F32R)
        w2p = m.sb("w2p", [P, 2, FC, D], F32R)
        xf = m.sb("xf", [P, 2, DC, GB, CAP])
        xp = m.sb("xp", [P, 2, 2, DC, GB * CAP], F32R)
        hf = m.sb("hf", [P, 2, S])
        hp = m.sb("hp", [P, 2, 2, FC, S], F32R)
        ys = m.sb("ys", [P, 2, GB, D])
        up = m.ps("up", [P, 4, S])
        yp = m.ps("yp", [P, 2, S])
        slot_col_d, slot_d, prob_d = routes
        slot_col = m.sb("slot_col", [P, 1])
        srow = m.sb("srow", [P, 2, GB, S], BF16)
        prow = m.sb("prow", [P, 2, GB, S])
        placed = m.sb("placed", [P, S])
        weight = m.sb("weight", [P, 2, GB])
        sums = m.sb("sums", [P, B * H * S // P])
        col_in = m.sem("col_in")
        rows_in = [m.sem(f"rows_in{s}") for s in range(2)]
        weighed = m.sem("weighed")
        sums_in = m.sem("sums_in")
        inverted = m.sem("inverted")
        inv_stored = m.sem("inv_stored")
        w1_in = m.sem("w1_in")
        w2_in = m.sem("w2_in")
        w1_high = m.sem("w1_high")
        w1_low = m.sem("w1_low")
        w2_high = m.sem("w2_high")
        w2_low = m.sem("w2_low")
        x_in = [m.sem(f"x_in{s}") for s in range(2)]
        x_high = m.sem("x_high")
        x_low = m.sem("x_low")
        up_full = m.sem("up_full")
        h_high = m.sem("h_high")
        h_full = m.sem("h_full")
        h_low = m.sem("h_low")
        y_full = m.sem("y_full")
        y_out = m.sem("y_out")
        y_stored = [m.sem(f"y_stored{s}") for s in range(2)]

        with nc.Block() as block:

            @block.sync
            def _(sp):
                def load_w(e):
                    wait_alone(sp, w1_low, e)
                    sp.dma_start(w1s[:, :, :], w1[bass.ds(e, 1)].rearrange("o (c p) f -> p (o c) f", p=P)).then_inc(w1_in, 16)
                    wait_alone(sp, w2_low, e)
                    sp.dma_start(w2s[:, :, :], w2[bass.ds(e, 1)].rearrange("o (c p) d -> p (o c) d", p=P)).then_inc(w2_in, 16)

                def load_x(e, g):
                    t = e * NG + g
                    wait_alone(sp, x_low, t - 1)
                    for c in range(DC):
                        sp.dma_start(xf[:, g % 2, c], xin_d[bass.ds(e, 1), g * GB:(g + 1) * GB, :, c].rearrange("o b p k -> p (o b) k")
                                     ).then_inc(x_in[g % 2], 16)

                def load_rows(e, g):
                    wait_alone(sp, weighed, (e * NG + g - 1) * GB)
                    for src, dst in ((slot_d, srow), (prob_d, prow)):
                        rows = src.rearrange("(b e) t -> b e t", e=NE)[g * GB:(g + 1) * GB, bass.ds(e, 1)]
                        sp.dma_start(dst[:, g % 2], rows.rearrange("b o t -> (b o) t").unsqueeze(0).to_broadcast([P, GB, S])
                                     ).then_inc(rows_in[g % 2], 16)

                def body(e):
                    last = isinstance(e, int) and e == NE - 1
                    for g in range(NG):
                        load_x(e, g)
                        load_rows(e, g)
                        if g == 4 and not last:
                            load_w(e + 1)
                        if g == 4 and isinstance(e, int) and e == 0:
                            sp.wait_ge(inverted, 1)
                            sp.dma_start(inv_d.rearrange(flat, g=P // B), sums[:, :]).then_inc(inv_stored, 16)

                load_w(0)
                sp.dma_start(slot_col[:, :], slot_col_d).then_inc(col_in, 16)
                flat = "b (g h) t -> (b g) (h t)"
                sp.dma_start(sums[:, :], sums_d.rearrange(flat, g=P // B)).then_inc(sums_in, 16)
                ends_apart(sp, NE, body)
                sp.wait_ge(inv_stored, 16)

            @block.gpsimd
            def _(pool):
                def body(e):
                    for g in range(NG):
                        t = e * NG + g
                        wait_alone(pool, y_out, (t + 1) * GB)
                        pool.dma_start(y_d[g * GB:(g + 1) * GB, :, bass.ds(e, 1), :].rearrange("b p o d -> p (b o) d"),
                                       ys[:, g % 2]).then_inc(y_stored[g % 2], 16)

                ends_apart(pool, NE, body)
                for s in range(2):
                    wait_alone(pool, y_stored[s], NE * NG // 2 * 16)

            @block.scalar
            def _(act):
                def split_w(stage, parts, arrived, done, used, e, when):
                    act.wait_ge(arrived, (e + 1) * 16)
                    wait(act, used, when)
                    act.activation(parts[:, 0], stage[:, :, :], ACT.Copy).then_inc(done, 1)

                def split_x(e, g):
                    t = e * NG + g
                    act.wait_ge(x_in[g % 2], (e * (NG // 2) + g // 2 + 1) * 32)
                    wait(act, up_full, (t - 1) * FC)
                    act.activation(xp[:, g % 2, 0], xf[:, g % 2].rearrange("p c b k -> p c (b k)"), ACT.Copy).then_inc(x_high, 1)

                def body(e):
                    last = isinstance(e, int) and e == NE - 1
                    split_w(w1s, w1p, w1_in, w1_high, up_full, e, e * (NG * FC))
                    for g in range(NG):
                        t = e * NG + g
                        for f in range(FC):
                            act.wait_ge(up_full, t * FC + f + 1)
                            if f == 0:
                                wait(act, y_full, (t - 1) * GB)
                            act.activation(hp[:, g % 2, 0, f], up[:, f % 4], ACT.Gelu_apprx_tanh).then_inc(h_high, 1)
                            wait(act, h_low, t * FC + f - 1)
                            act.activation(hf[:, f % 2], up[:, f % 4], ACT.Gelu_apprx_tanh).then_inc(h_full, 1)
                            if f == 2 and not (last and g == NG - 1):
                                split_x(e, g + 1)
                        if g == 0:
                            split_w(w2s, w2p, w2_in, w2_high, y_full, e, e * (NG * GB))

                split_x(0, 0)
                ends_apart(act, NE, body)

            @block.vector
            def _(dve):
                def split_x(e, g):
                    t = e * NG + g
                    dve.wait_ge(x_high, t + 1)
                    dve.tensor_tensor(xp[:, g % 2, 1], xf[:, g % 2].rearrange("p c b k -> p c (b k)"),
                                      xp[:, g % 2, 0].bitcast(F32), ALU.subtract).then_inc(x_low, 1)

                def y_evacuate(e, g, k):
                    t = e * NG + g
                    dve.wait_ge(y_full, t * GB + k + 1)
                    if k == 0:
                        wait(dve, y_stored[g % 2], (e * (NG // 2) + g // 2) * 16)
                    dve.wait_ge(weighed, t * GB + k + 1)
                    dve.tensor_scalar(ys[:, g % 2, k], yp[:, k % 2, 0:D], weight[:, g % 2, k:k + 1], None, ALU.mult).then_inc(y_out, 1)

                def weigh(e, g, k):
                    if k == 0:
                        dve.wait_ge(rows_in[g % 2], (e * (NG // 2) + g // 2 + 1) * 32)
                    wait(dve, weighed, (e * NG + g) * GB + k)
                    dve.scalar_tensor_tensor(placed[:, :], srow[:, g % 2, k], slot_col[:, 0:1], prow[:, g % 2, k],
                                             ALU.is_equal, ALU.mult, accum_out=weight[:, g % 2, k:k + 1]).then_inc(weighed, 1)

                def body(e):
                    first = isinstance(e, int) and e == 0
                    last = isinstance(e, int) and e == NE - 1
                    dve.wait_ge(w1_high, e + 1)
                    dve.tensor_tensor(w1p[:, 1], w1s[:, :, :], w1p[:, 0].bitcast(F32), ALU.subtract).then_inc(w1_low, 1)
                    for g in range(NG):
                        t = e * NG + g
                        for f in range(FC):
                            dve.wait_ge(h_full, t * FC + f + 1)
                            dve.tensor_tensor(hp[:, g % 2, 1, f], hf[:, f % 2], hp[:, g % 2, 0, f].bitcast(F32),
                                              ALU.subtract).then_inc(h_low, 1)
                            if f == 2 and not (last and g == NG - 1):
                                split_x(e, g + 1)
                            if f % 2 and not (first and g == 0):
                                y_evacuate(e, g - 1, f // 2)
                            if f % 2 == 0:
                                weigh(e, g, f // 2)
                        if g == 0:
                            dve.wait_ge(w2_high, e + 1)
                            dve.tensor_tensor(w2p[:, 1], w2s[:, :, :], w2p[:, 0].bitcast(F32), ALU.subtract).then_inc(w2_low, 1)
                        if g == 1 and first:
                            dve.wait_ge(sums_in, 16)
                            dve.reciprocal(sums[:, :], sums[:, :]).then_inc(inverted, 1)

                dve.wait_ge(col_in, 16)
                split_x(0, 0)
                ends_apart(dve, NE, body)
                for k in range(GB):
                    y_evacuate(NE, -1, k)

            @block.tensor
            def _(pe):
                def down(e, g, k, half):
                    t = e * NG + g
                    if half == 0:
                        if k == 0:
                            pe.wait_ge(h_low, (t + 1) * FC)
                            pe.wait_ge(w2_low, e + (1 if g >= 0 else 0))
                        wait(pe, y_out, t * GB + k - 1)
                    for f in range(4 * half, 4 * half + 4):
                        for s, (hi, wi) in enumerate(SPLITS):
                            ins = pe.matmul(yp[:, k % 2, 0:D], hp[:, g % 2, hi, f, k * CAP:(k + 1) * CAP], w2p[:, wi, f, :],
                                            start=(f == 0 and s == 0), stop=(f == FC - 1 and s == 2))
                    if half == 1:
                        ins.then_inc(y_full, 1)

                def body(e):
                    first = isinstance(e, int) and e == 0
                    pe.wait_ge(w1_low, e + 1)
                    for g in range(NG):
                        t = e * NG + g
                        pe.wait_ge(x_low, t + 1)
                        for f in range(FC):
                            wait(pe, h_full, t * FC + f - 3)
                            for s, (wi, xi) in enumerate(SPLITS):
                                for c in range(DC):
                                    ins = pe.matmul(up[:, f % 4, :], w1p[:, wi, c, f * P:(f + 1) * P], xp[:, g % 2, xi, c, :],
                                                    start=(s == 0 and c == 0), stop=(s == 2 and c == DC - 1))
                            ins.then_inc(up_full, 1)
                            if not (first and g == 0):
                                down(e, g - 1, f // 2, f % 2)

                ends_apart(pe, NE, body)
                for k in range(GB):
                    down(NE, -1, k, 0)
                    down(NE, -1, k, 1)


def combine_phase(nc, x, Wo, bo, slot_col_d, slot_d, y_d, att_d, inv_d, out):
    with ExitStack() as ctx:
        m = Memory(nc, ctx, "out")
        wo = m.sb("wo", [P, DC, D])
        bob = m.sb("bob", [P, D])
        slot_col = m.sb("slot_col", [P, 1])
        srow = m.sb("srow", [P, 2, NE, S], BF16)
        hot = m.sb("hot", [P, 2, NE, S], F32R)
        y = m.sb("y", [P, 2, NE, D])
        yh = m.sb("yh", [P, 2, 2, NE, D], F32R)
        att = m.sb("att", [P, 2, DC, S])
        inv = m.sb("inv", [P, 2, DC, S])
        xi = m.sb("xi", [P, 2, TT, D])
        xb = m.sb("xb", [P, 2, TT, D])
        ffn = m.sb("ffn", [P, 2, TT, D], BF16)
        res = m.sb("res", [P, 2, TT, D])
        ap = m.ps("ap", [P, 2, 2, 2, D])
        fp = m.ps("fp", [P, 4, 2, D])
        const_in = m.sem("const_in")
        rows_in = [m.sem(f"rows_in{s}") for s in range(2)]
        y_in = [m.sem(f"y_in{s}") for s in range(2)]
        b_in = [m.sem(f"b_in{s}") for s in range(2)]
        placed = m.sem("placed")
        y_high = m.sem("y_high")
        y_low = m.sem("y_low")
        divided = m.sem("divided")
        a_full = m.sem("a_full")
        f_full = m.sem("f_full")
        a_out = m.sem("a_out")
        f_out = m.sem("f_out")
        biased = m.sem("biased")
        summed = m.sem("summed")
        stored = [m.sem(f"stored{s}") for s in range(2)]

        with nc.Block() as block:

            @block.sync
            def _(sp):
                sp.dma_start(slot_col[:, :], slot_col_d).then_inc(const_in, 16)
                sp.dma_start(wo[:, :, :], Wo.rearrange("(c p) n -> p c n", p=P)).then_inc(const_in, 16)
                sp.dma_start(bob[:, :], bo.partition_broadcast(P)).then_inc(const_in, 16)

                def body(i):
                    for s in range(2):
                        b = i * 2 + s
                        wait_alone(sp, y_low, b - 1)
                        sp.dma_start(y[:, s], y_d[bass.ds(b, 1)].rearrange("o p e d -> p (o e) d")).then_inc(y_in[s], 16)
                        wait_alone(sp, a_full, (b - 1) * 2)
                        sp.dma_start(att[:, s], att_d[bass.ds(b, 1)].rearrange("o (c p) t -> p (o c) t", p=P)).then_inc(b_in[s], 16)
                        for c in range(DC):
                            heads = inv_d[bass.ds(b, 1), c * (H // DC):(c + 1) * (H // DC)]
                            sp.dma_start(inv[:, s, c], heads.rearrange("o h t -> (o h) t").unsqueeze(1).to_broadcast([H // DC, HD, S])
                                         ).then_inc(b_in[s], 16)
                        wait_alone(sp, biased, b - 1)
                        sp.dma_start(xi[:, s], x[bass.ds(b, 1)].rearrange("o (t p) d -> p (o t) d", p=P)).then_inc(b_in[s], 16)

                first_apart(sp, B // 2, body)

            @block.gpsimd
            def _(pool):
                def load_rows(b, s):
                    wait_alone(pool, placed, (b - 1) * NE)
                    pool.dma_start(srow[:, s], slot_d[bass.ds(b * NE, NE)].rearrange("e t -> (e t)").partition_broadcast(P)
                                   .rearrange("p (e t) -> p e t", e=NE)).then_inc(rows_in[s], 16)

                load_rows(0, 0)
                pool.wait_ge(const_in, 48)

                def body(i):
                    last = isinstance(i, int) and i == B // 2 - 1
                    for s in range(2):
                        b = i * 2 + s
                        if not (last and s):
                            load_rows(b + 1, 1 - s)
                        wait_alone(pool, b_in[s], (i + 1) * 64)
                        pool.tensor_tensor(att[:, s], att[:, s], inv[:, s], ALU.mult).then_inc(divided, 1)
                        wait_alone(pool, a_out, (b - 1) * 2)
                        pool.tensor_tensor(xb[:, s], xi[:, s], bob[:, :].unsqueeze(1).to_broadcast([P, TT, D]), ALU.add).then_inc(biased, 1)

                ends_apart(pool, B // 2, body)

            @block.vector
            def _(dve):
                dve.wait_ge(const_in, 48)

                def finish(b, s, turn):
                    dve.wait_ge(biased, b + 1)
                    wait(dve, stored[s], turn * 16)
                    for k in range(2):
                        dve.wait_ge(a_full, b * 2 + k + 1)
                        dve.tensor_tensor(res[:, s, 2 * k:2 * k + 2], ap[:, s, k], xb[:, s, 2 * k:2 * k + 2], ALU.add).then_inc(a_out, 1)
                    dve.wait_ge(a_out, b * 2 + 2)
                    for k in range(2):
                        dve.wait_ge(f_out, b * 2 + k + 1)
                        dve.tensor_tensor(res[:, s, 2 * k:2 * k + 2], res[:, s, 2 * k:2 * k + 2],
                                          ffn[:, s, 2 * k:2 * k + 2], ALU.add).then_inc(summed, 1)

                def body(i):
                    for s in range(2):
                        b = i * 2 + s
                        dve.wait_ge(rows_in[s], (i + 1) * 16)
                        wait(dve, f_full, (b - 1) * 2)
                        for e in range(NE):
                            dve.tensor_scalar(hot[:, s, e], srow[:, s, e], slot_col[:, 0:1], None, ALU.is_equal).then_inc(placed, 1)
                        dve.wait_ge(y_high, b + 1)
                        dve.tensor_tensor(yh[:, s, 1], y[:, s], yh[:, s, 0].bitcast(F32), ALU.subtract).then_inc(y_low, 1)
                        if not (isinstance(i, int) and b == 0):
                            finish(b - 1, 1 - s, i + s - 1)

                first_apart(dve, B // 2, body)
                finish(B - 1, 1, B // 2 - 1)

            @block.scalar
            def _(act):
                def evacuate(b, s):
                    wait(act, summed, (b - 1) * 2)
                    for k in range(2):
                        act.wait_ge(f_full, b * 2 + k + 1)
                        act.activation(ffn[:, s, 2 * k:2 * k + 2], fp[:, 2 * s + k], ACT.Copy).then_inc(f_out, 1)

                def store(b, s):
                    act.wait_ge(summed, (b + 1) * 2)
                    act.dma_start(out[bass.ds(b, 1)].rearrange("o (t p) d -> p (o t) d", p=P), res[:, s]).then_inc(stored[s], 16)

                def body(i):
                    first = isinstance(i, int)
                    for s in range(2):
                        b = i * 2 + s
                        act.wait_ge(y_in[s], (i + 1) * 16)
                        wait(act, f_full, (b - 1) * 2)
                        act.activation(yh[:, s, 0], y[:, s], ACT.Copy).then_inc(y_high, 1)
                        if not (first and b == 0):
                            evacuate(b - 1, 1 - s)
                        if not first:
                            store(b - 2, s)

                first_apart(act, B // 2, body)
                evacuate(B - 1, 1)
                store(B - 2, 0)
                store(B - 1, 1)
                for s in range(2):
                    act.wait_ge(stored[s], B // 2 * 16)

            @block.tensor
            def _(pe):
                pe.wait_ge(const_in, 48)

                def body(i):
                    for s in range(2):
                        b = i * 2 + s
                        pe.wait_ge(b_in[s], (i + 1) * 64)
                        pe.wait_ge(divided, b + 1)
                        wait(pe, a_out, (b - 1) * 2)
                        for k in range(2):
                            for t in range(2):
                                tok = (2 * k + t) * P
                                for c in range(DC):
                                    ins = pe.matmul(ap[:, s, k, t], att[:, s, c, tok:tok + P], wo[:, c], start=(c == 0), stop=(c == DC - 1))
                            ins.then_inc(a_full, 1)
                        wait(pe, f_out, (b - 1) * 2)
                        pe.wait_ge(placed, (b + 1) * NE)
                        pe.wait_ge(y_low, b + 1)
                        for k in range(2):
                            for t in range(2):
                                tok = (2 * k + t) * P
                                for e in range(NE):
                                    for part in range(2):
                                        ins = pe.matmul(fp[:, 2 * s + k, t], hot[:, s, e, tok:tok + P], yh[:, s, part, e],
                                                        start=(e == 0 and part == 0), stop=(e == NE - 1 and part == 1))
                            ins.then_inc(f_full, 1)

                first_apart(pe, B // 2, body)


def build(nc, x, Wq, bq, Wk, bk, Wv, bv, Wp, bp, Wo, bo, u, v, gate_w, w1, w2, out):
    names = ("sinusoid", "ident", "slots", "slot_col", "keep")
    c = {n: nc.inline_tensor(a, name=f"const_{n}").ap() for n, a in zip(names, shape_constants())}
    xn_d = nc.dram_tensor("xn_d", [B, P, TT, D], F32).ap()
    xt_d = nc.dram_tensor("xt_d", [B, P, 2, DC, S], F32).ap()
    slot_d = nc.dram_tensor("slot_d", [B * NE, S], BF16).ap()
    prob_d = nc.dram_tensor("prob_d", [B * NE, S], F32).ap()
    xin_d = nc.dram_tensor("xin_d", [NE, B, P, DC, CAP], F32).ap()
    y_d = nc.dram_tensor("y_d", [B, CAP, NE, D], F32).ap()
    xs_d = nc.dram_tensor("xs_d", [4, S * (S + 1)], F32).ap()
    att_d = nc.dram_tensor("att_d", [B, D, S], F32).ap()
    sums_d = nc.dram_tensor("sums_d", [B, H, S], F32).ap()
    inv_d = nc.dram_tensor("inv_d", [B, H, S], F32).ap()
    with nc.sbuf_tensor("slot_t", [P, B, TT, NE], F32) as slot_t:
        with nc.sbuf_tensor("gate_scores", [P, B, TT, NE], F32) as gate:
            norm_phase(nc, x, gate_w, c["ident"], xn_d, xt_d, gate)
            route_phase(nc, c["ident"], gate, slot_t, slot_d, prob_d)
        gather_phase(nc, c["slots"], slot_t, xn_d, xin_d)
    weights = {"Wq": Wq, "Wk": Wk, "Wv": Wv, "Wp": Wp, "bq": bq, "bk": bk, "bv": bv, "bp": bp,
               "u": u.rearrange("a h b p -> (a h b p)"), "v": v.rearrange("a h b p -> (a h b p)")}
    attention_phase(nc, weights, (c["sinusoid"], c["ident"], c["keep"]), xt_d, xs_d, att_d, sums_d)
    ffn_phase(nc, w1, w2, xin_d, (c["slot_col"], slot_d, prob_d), y_d, sums_d, inv_d)
    combine_phase(nc, x, Wo, bo, c["slot_col"], slot_d, y_d, att_d, inv_d, out)


_INS = ["L0_attn_x", "L0_attn_Wq", "L0_attn_bq", "L0_attn_Wk", "L0_attn_bk", "L0_attn_Wv", "L0_attn_bv", "L0_attn_Wp",
        "L0_attn_bp", "L0_attn_Wo", "L0_attn_bo", "L0_attn_u", "L0_attn_v", "L0_ffn_gate_w", "L0_ffn_w1", "L0_ffn_w2"]
_OUTS = [((B, S, D), "float32")]


def kernel(**inputs):
    import numpy as _np
    import concourse.bacc as _bacc
    from concourse import mybir as _mybir
    from concourse.bass_utils import run_bass_kernel_spmd as _run

    nc = _bacc.Bacc("TRN2", target_bir_lowering=False, num_devices=1)
    arrays, args = {}, []
    for name in _INS:
        a = _np.ascontiguousarray(inputs[name])
        arrays[f"in_{name}_dram"] = a
        args.append(nc.dram_tensor(f"in_{name}_dram", a.shape, _mybir.dt.from_np(a.dtype), kind="ExternalInput").ap())
    for i, (shape, dtype) in enumerate(_OUTS):
        dt = _mybir.dt.from_np(_np.dtype(dtype))
        args.append(nc.dram_tensor(f"out_{i}_dram", shape, dt, kind="ExternalOutput").ap())
    build(nc, *args)
    r = _run(nc, [arrays], core_ids=[0])
    got = tuple(r.results[0][f"out_{i}_dram"] for i in range(len(_OUTS)))
    return got[0]
```
